# Optimizing a Trainium2 kernel written in Bass

```python
import numpy as np
import jax
import jax.numpy as jnp

def _softmax(x, axis=-1):
    return jax.nn.softmax(x, axis=axis)

def _gelu(x):
    return jax.nn.gelu(x, approximate=True)

def _silu(x):
    return jax.nn.silu(x)

def _sigmoid(x):
    return jax.nn.sigmoid(x)

def _layernorm(x, axis=-1, eps=1e-05):
    m = jnp.mean(x, axis=axis, keepdims=True)
    v = jnp.var(x, axis=axis, keepdims=True)
    return (x - m) / jnp.sqrt(v + eps)

def _scatter_add(tgt, idx, src, axis=0):
    return tgt.at[idx].add(src)

def _segment_sum(src, seg, n):
    return jax.ops.segment_sum(src, seg, n)
kernel_name = 'mk_conv_seq_d1_conv_nchw256_r4_8aa79f'

def setup_inputs(seed: int=0):
    np.random.seed(seed)
    _w = jnp.asarray

    def _rec_inputs():
        import jax
        import jax.numpy as jnp
        _gk = jax.random.key(seed)
        x = -0.0003929 + 0.9999 * jax.random.normal(jax.random.fold_in(_gk, 1), (16, 64, 16, 16), jnp.float32)
        return x
    x = _rec_inputs()

    def _L0_conv_setup():
        import jax, jax.numpy as jnp
        import numpy as np
        C = 64
        HEADS = 8
        WIN = 8
        SHIFT = 4
        HIDDEN = int(C * 4.0)
        EPS = 1e-06

        def _ln2d(x, g, b):
            mu = jnp.mean(x, axis=1, keepdims=True)
            var = jnp.mean(jnp.square(x - mu), axis=1, keepdims=True)
            xh = (x - mu) * jax.lax.rsqrt(var + EPS)
            return xh * g[None, :, None, None] + b[None, :, None, None]

        def _window_partition(x, win):
            b, c, h, w = x.shape
            x = x.reshape(b, c, h // win, win, w // win, win)
            x = jnp.transpose(x, (0, 2, 4, 3, 5, 1))
            return x.reshape(-1, win * win, c)

        def _window_reverse(windows, win, h, w, b):
            c = windows.shape[-1]
            x = windows.reshape(b, h // win, w // win, win, win, c)
            x = jnp.transpose(x, (0, 5, 1, 3, 2, 4))
            return x.reshape(b, c, h, w)

        def _mha(x, in_w, in_b, out_w, out_b):
            nw, L, c = x.shape
            dh = c // HEADS
            qkv = x @ in_w.T + in_b
            q, k, v = jnp.split(qkv, 3, axis=-1)
            reshape_h = lambda t: t.reshape(nw, L, HEADS, dh).transpose(0, 2, 1, 3)
            q, k, v = (reshape_h(q), reshape_h(k), reshape_h(v))
            scores = jnp.einsum('nhid,nhjd->nhij', q, k) / jnp.sqrt(jnp.float32(dh)).astype(x.dtype)
            attn = jax.nn.softmax(scores, axis=-1)
            out = jnp.einsum('nhij,nhjd->nhid', attn, v)
            out = out.transpose(0, 2, 1, 3).reshape(nw, L, c)
            return out @ out_w.T + out_b
        key = jax.random.key(seed)
        ks = jax.random.split(key, 16)
        s = lambda fan: 1.0 / np.sqrt(fan)
        return {'x': jax.random.normal(ks[0], (16, C, 16, 16), jnp.float32), 'norm1_g': jnp.ones((C,), jnp.float32), 'norm1_b': jnp.zeros((C,), jnp.float32), 'in_w': jax.random.normal(ks[1], (3 * C, C), jnp.float32) * s(C), 'in_b': jnp.zeros((3 * C,), jnp.float32), 'out_w': jax.random.normal(ks[2], (C, C), jnp.float32) * s(C), 'out_b': jnp.zeros((C,), jnp.float32), 'proj_w': jax.random.normal(ks[3], (C, C), jnp.float32) * s(C), 'proj_b': jnp.zeros((C,), jnp.float32), 'norm2_g': jnp.ones((C,), jnp.float32), 'norm2_b': jnp.zeros((C,), jnp.float32), 'fc1_w': jax.random.normal(ks[4], (HIDDEN, C), jnp.float32) * s(C), 'fc1_b': jnp.zeros((HIDDEN,), jnp.float32), 'fc2_w': jax.random.normal(ks[5], (C, HIDDEN), jnp.float32) * s(HIDDEN), 'fc2_b': jnp.zeros((C,), jnp.float32)}
    _L0_conv_all = _L0_conv_setup()
    _L0_conv_in = {k: v for k, v in _L0_conv_all.items() if k in ('norm1_g', 'norm1_b', 'in_w', 'in_b', 'out_w', 'out_b', 'proj_w', 'proj_b', 'norm2_g', 'norm2_b', 'fc1_w', 'fc1_b', 'fc2_w', 'fc2_b')}
    del _L0_conv_all
    return {'x': x, 'L0_conv_norm1_g': _L0_conv_in['norm1_g'], 'L0_conv_norm1_b': _L0_conv_in['norm1_b'], 'L0_conv_in_w': _L0_conv_in['in_w'], 'L0_conv_in_b': _L0_conv_in['in_b'], 'L0_conv_out_w': _L0_conv_in['out_w'], 'L0_conv_out_b': _L0_conv_in['out_b'], 'L0_conv_proj_w': _L0_conv_in['proj_w'], 'L0_conv_proj_b': _L0_conv_in['proj_b'], 'L0_conv_norm2_g': _L0_conv_in['norm2_g'], 'L0_conv_norm2_b': _L0_conv_in['norm2_b'], 'L0_conv_fc1_w': _L0_conv_in['fc1_w'], 'L0_conv_fc1_b': _L0_conv_in['fc1_b'], 'L0_conv_fc2_w': _L0_conv_in['fc2_w'], 'L0_conv_fc2_b': _L0_conv_in['fc2_b']}

def reference(x, L0_conv_norm1_g, L0_conv_norm1_b, L0_conv_in_w, L0_conv_in_b, L0_conv_out_w, L0_conv_out_b, L0_conv_proj_w, L0_conv_proj_b, L0_conv_norm2_g, L0_conv_norm2_b, L0_conv_fc1_w, L0_conv_fc1_b, L0_conv_fc2_w, L0_conv_fc2_b):
    import jax
    import jax.numpy as jnp

    def _L0_conv_ref(x, norm1_g, norm1_b, in_w, in_b, out_w, out_b, proj_w, proj_b, norm2_g, norm2_b, fc1_w, fc1_b, fc2_w, fc2_b):
        import jax, jax.numpy as jnp
        import numpy as np
        C = 64
        HEADS = 8
        WIN = 8
        SHIFT = 4
        HIDDEN = int(C * 4.0)
        EPS = 1e-06

        def _ln2d(x, g, b):
            mu = jnp.mean(x, axis=1, keepdims=True)
            var = jnp.mean(jnp.square(x - mu), axis=1, keepdims=True)
            xh = (x - mu) * jax.lax.rsqrt(var + EPS)
            return xh * g[None, :, None, None] + b[None, :, None, None]

        def _window_partition(x, win):
            b, c, h, w = x.shape
            x = x.reshape(b, c, h // win, win, w // win, win)
            x = jnp.transpose(x, (0, 2, 4, 3, 5, 1))
            return x.reshape(-1, win * win, c)

        def _window_reverse(windows, win, h, w, b):
            c = windows.shape[-1]
            x = windows.reshape(b, h // win, w // win, win, win, c)
            x = jnp.transpose(x, (0, 5, 1, 3, 2, 4))
            return x.reshape(b, c, h, w)

        def _mha(x, in_w, in_b, out_w, out_b):
            nw, L, c = x.shape
            dh = c // HEADS
            qkv = x @ in_w.T + in_b
            q, k, v = jnp.split(qkv, 3, axis=-1)
            reshape_h = lambda t: t.reshape(nw, L, HEADS, dh).transpose(0, 2, 1, 3)
            q, k, v = (reshape_h(q), reshape_h(k), reshape_h(v))
            scores = jnp.einsum('nhid,nhjd->nhij', q, k) / jnp.sqrt(jnp.float32(dh)).astype(x.dtype)
            attn = jax.nn.softmax(scores, axis=-1)
            out = jnp.einsum('nhij,nhjd->nhid', attn, v)
            out = out.transpose(0, 2, 1, 3).reshape(nw, L, c)
            return out @ out_w.T + out_b
        shortcut = x
        xn = _ln2d(x, norm1_g, norm1_b)
        b, c, h, w = xn.shape
        win = min(WIN, h, w)
        pad_h = (win - h % win) % win
        pad_w = (win - w % win) % win
        if pad_h or pad_w:
            xn = jnp.pad(xn, ((0, 0), (0, 0), (0, pad_h), (0, pad_w)))
        hp, wp = (xn.shape[2], xn.shape[3])
        shifted = 0 < SHIFT < win
        if shifted:
            xn = jnp.roll(xn, shift=(-SHIFT, -SHIFT), axis=(2, 3))
        windows = _window_partition(xn, win)
        attn_out = _mha(windows, in_w, in_b, out_w, out_b)
        attn_out = attn_out @ proj_w.T + proj_b
        y = _window_reverse(attn_out, win, hp, wp, b)
        if shifted:
            y = jnp.roll(y, shift=(SHIFT, SHIFT), axis=(2, 3))
        if pad_h or pad_w:
            y = y[:, :, :h, :w]
        y = shortcut + y
        z = _ln2d(y, norm2_g, norm2_b)
        z = jnp.einsum('bchw,oc->bohw', z, fc1_w) + fc1_b[None, :, None, None]
        z = jax.nn.gelu(z, approximate=False)
        z = jnp.einsum('bchw,oc->bohw', z, fc2_w) + fc2_b[None, :, None, None]
        return y + z

    def _gn(v, G=32, eps=1e-05):
        B_, C_, H_, W_ = v.shape
        g = v.reshape(B_, G, C_ // G, H_, W_)
        m = jnp.mean(g, axis=(2, 3, 4), keepdims=True)
        s = jnp.var(g, axis=(2, 3, 4), keepdims=True)
        return ((g - m) / jnp.sqrt(s + eps)).reshape(v.shape)

    def _ln_c(v, eps=1e-06):
        m = jnp.mean(v, axis=1, keepdims=True)
        s = jnp.var(v, axis=1, keepdims=True)
        return (v - m) / jnp.sqrt(s + eps)

    def _ln_t(v, eps=1e-05):
        m = jnp.mean(v, axis=-1, keepdims=True)
        s = jnp.var(v, axis=-1, keepdims=True)
        return (v - m) / jnp.sqrt(s + eps)

    def _to_tokens(v):
        B_, C_, H_, W_ = v.shape
        return v.reshape(B_, C_, H_ * W_).transpose(0, 2, 1)

    def _from_tokens(t, like):
        B_, C_, H_, W_ = like.shape
        return t.transpose(0, 2, 1).reshape(B_, C_, H_, W_)
    x = _L0_conv_ref(x, L0_conv_norm1_g, L0_conv_norm1_b, L0_conv_in_w, L0_conv_in_b, L0_conv_out_w, L0_conv_out_b, L0_conv_proj_w, L0_conv_proj_b, L0_conv_norm2_g, L0_conv_norm2_b, L0_conv_fc1_w, L0_conv_fc1_b, L0_conv_fc2_w, L0_conv_fc2_b)
    return x

_drawn_inputs = setup_inputs


def setup_inputs(seed=0):
    import zlib

    import numpy as np

    out = dict(_drawn_inputs(seed))
    spreads = {'L0_conv_norm1_g': (1.0, 0.2),
     'L0_conv_norm1_b': (0.0, 0.1),
     'L0_conv_in_b': (0.0, 0.1),
     'L0_conv_out_b': (0.0, 0.1),
     'L0_conv_proj_b': (0.0, 0.1),
     'L0_conv_norm2_g': (1.0, 0.2),
     'L0_conv_norm2_b': (0.0, 0.1),
     'L0_conv_fc1_b': (0.0, 0.1),
     'L0_conv_fc2_b': (0.0, 0.1)}
    factors = {}
    for name, (base, spread) in spreads.items():
        noise = np.random.default_rng([zlib.crc32(name.encode()), seed]).standard_normal(out[name].shape)
        drawn = base * np.exp(spread * noise) if base else spread * noise
        out[name] = jnp.asarray(drawn.astype(out[name].dtype))
    for name, factor in factors.items():
        out[name] = (out[name] * factor).astype(out[name].dtype)
    return out
```

```python
from contextlib import ExitStack

import numpy as np

import concourse.bass as bass
from concourse import mybir

F32 = mybir.dt.float32
ALU = mybir.AluOpType
ACT = mybir.ActivationFunctionType
AX = mybir.AxisListType

B, C, HH, WW = 16, 64, 16, 16
WIN, SHIFT = 8, 4
HEADS = 8
D = C // HEADS
HIDDEN = 4 * C
EPS = 1e-6
P = 128
TOK = HH * WW
TILES = B // 2
L = WIN * WIN
PAIRS = TOK // L
BLK = TOK // P
GRP = BLK * 2
M2 = HIDDEN // P
STEP = 2 * TOK
STEPS = TILES // 2
ALL = TILES * TOK
NV = 12
G1, B1, BQ, OUTB, PROJB, G2, B2, FC2B, FC1B = 0, 1, 2, 5, 6, 7, 8, 9, 10
NM = 12
EARLY = P + NM + NV + 3 * C
LATE = P + HIDDEN + M2 * C + 2 * P


def swin_block_kernel(nc, x_tok_d, x_ch_d, early_d, late_d, out_d):
    ctx = ExitStack()
    with ctx:
        def sb(name, shape):
            return ctx.enter_context(nc.sbuf_tensor(name, shape, F32))

        def bank(name):
            return ctx.enter_context(nc.psum_tensor(name, [P, 512], F32))

        def sem(name):
            return ctx.enter_context(nc.semaphore(name))

        x_tok = sb("x_tok", [P, ALL])
        x_ch = sb("x_ch", [P, ALL])
        early = sb("early", [P, EARLY])
        late = sb("late", [P, LATE])
        ident = early[:, 0:P]
        half_mask = early[:, P:P + 2]
        head_mask = early[:, P + 2:P + 2 + HEADS]
        row_mask = early[:, P + 10:P + 12]
        vec = early[:, P + NM:P + NM + NV]
        w_in_t = early[:, P + NM + NV:EARLY]
        perm_v = late[:, 0:P]
        w_fc1_t = late[:, P:P + HIDDEN]
        w_fc2_t = late[:, P + HIDDEN:P + HIDDEN + M2 * C]
        out_w_x = late[0:C, LATE - 2 * P:LATE - P]
        proj_w_t = late[0:C, LATE - P:LATE]

        w_qkv = sb("w_qkv", [P, 3, P])
        b_qkv = sb("b_qkv", [P, 4])
        w_out = sb("w_out", [P, 2, C])
        b_out = sb("b_out", [P, 1])
        w_fc1 = sb("w_fc1", [P, 2, HIDDEN])
        b_fc1 = sb("b_fc1", [P, M2])

        stats1 = sb("stats1", [P, 2, GRP, 6])
        mv1 = sb("mv1", [P, 2, GRP, 2])
        var1 = sb("var1", [P, 2, GRP])
        rstd1 = sb("rstd1", [P, 2, GRP])
        stats2 = sb("stats2", [P, 2, GRP, 6])
        mv2 = sb("mv2", [P, 2, GRP, 2])
        var2 = sb("var2", [P, 2, GRP])
        rstd2 = sb("rstd2", [P, 2, GRP])
        minus_half = sb("minus_half", [P, GRP])
        xhat = sb("xhat", [P, 2, TOK])
        zhat = sb("zhat", [P, 2, TOK])

        xn = sb("xn", [P, 2, TOK])
        q_bd = sb("q_bd", [P, 2, PAIRS, P])
        k_ch = sb("k_ch", [P, 2, TOK])
        k_mask = sb("k_mask", [P, 2, PAIRS, HEADS, L])
        v_ch = sb("v_ch", [P, PAIRS, 2, L])
        v_z = sb("v_z", [P, 2, PAIRS, P])
        row_max = sb("row_max", [P, 2, HEADS])
        shifted = sb("shifted", [P, 2, 512])
        probs = sb("probs", [P, 2, 512])
        probs_t = sb("probs_t", [P, 2, 512])
        row_sum = sb("row_sum", [P, 2, PAIRS, HEADS])
        recip = sb("recip", [P, PAIRS * HEADS])
        recip_x = sb("recip_x", [P, PAIRS * HEADS, 2 * D])
        recip_t = sb("recip_t", [P, 512])
        attn = sb("attn", [P, PAIRS, 2, L])
        y_tile = sb("y_tile", [P, 2, TOK])
        y_all = sb("y_all", [P, ALL])
        z_all = sb("z_all", [P, ALL])

        hidden = sb("hidden", [P, 2, 4, STEP])
        result = sb("result", [P, 2, STEP])

        ps_s = [bank("ps_s0"), bank("ps_s1")]
        ps_pt = bank("ps_pt")
        ps_u = [bank("ps_u0"), bank("ps_u1")]
        ps_m0, ps_m1, ps_m2 = bank("ps_m0"), bank("ps_m1"), bank("ps_m2")
        ps_h = [ps_s[0], ps_s[1], ps_pt, ps_m0]
        ps_f = ps_u

        s_early, s_late = sem("s_early"), sem("s_late")
        s_xtok, s_xch = [sem(f"s_xtok{i}") for i in range(4)], sem("s_xch")
        s_zero, s_wqkv, s_bps, s_bias, s_lps, s_latew = (
            sem("s_zero"), sem("s_wqkv"), sem("s_bps"), sem("s_bias"), sem("s_lps"), sem("s_latew"))
        s_st1, s_mv1, s_var1, s_rstd1, s_xhat, s_x1, s_xn = (
            sem("s_st1"), sem("s_mv1"), sem("s_var1"), sem("s_rstd1"), sem("s_xhat"), sem("s_x1"), sem("s_xn"))
        s_qk, s_qkch, s_kmask, s_v, s_vch, s_vt, s_vz = (
            sem("s_qk"), sem("s_qkch"), sem("s_kmask"), sem("s_v"), sem("s_vch"), sem("s_vt"), sem("s_vz"))
        s_scores, s_max, s_shift, s_exp, s_sum, s_pt, s_ptsb, s_pv = (
            sem("s_scores"), sem("s_max"), sem("s_shift"), sem("s_exp"), sem("s_sum"), sem("s_pt"),
            sem("s_ptsb"), sem("s_pv"))
        s_recip, s_recx, s_r, s_rsb, s_attn, s_proj, s_y, s_ycopy, s_yt = (
            sem("s_recip"), sem("s_recx"), sem("s_r"), sem("s_rsb"), sem("s_attn"), sem("s_proj"),
            sem("s_y"), sem("s_ycopy"), sem("s_yt"))
        s_st2, s_mv2, s_var2, s_rstd2, s_zhat, s_zt, s_z = (
            sem("s_st2"), sem("s_mv2"), sem("s_var2"), sem("s_rstd2"), sem("s_zhat"), sem("s_zt"), sem("s_z"))
        s_fc1, s_gelu, s_fc2, s_res = sem("s_fc1"), sem("s_gelu"), sem("s_fc2"), sem("s_res")
        s_out = [sem(f"s_out{s}") for s in range(STEPS)]

        XTOK = [(0, 1), (1, 2), (2, 4), (4, 8)]

        def xtok_load(k):
            return next(i for i, (a, b) in enumerate(XTOK) if a <= k < b)

        def tile_ok(k):
            return 0 <= k < TILES

        block = ctx.enter_context(nc.Block())

        @block.sync
        def _(sp):
            a, b = XTOK[0]
            sp.dma_start(x_tok[:, a * TOK:b * TOK], x_tok_d[:, a * TOK:b * TOK]).then_inc(s_xtok[0], 16)
            for i in range(1, 4):
                a, b = XTOK[i]
                sp.dma_start(x_tok[:, a * TOK:b * TOK], x_tok_d[:, a * TOK:b * TOK]).then_inc(s_xtok[i], 16)
            sp.dma_start(late[:], late_d).then_inc(s_late, 16)
            sp.dma_start(x_ch[:], x_ch_d).then_inc(s_xch, 16)
            for s in range(STEPS):
                sp.wait_ge(s_res, s + 1)
                sp.dma_start(out_d[:, s * STEP:(s + 1) * STEP], result[:, s % 2, :]).then_inc(s_out[s], 16)
            for s in range(STEPS):
                sp.wait_ge(s_out[s], 16)

        @block.tensor
        def _(pe):
            def scores(g):
                k, p = g // PAIRS, g % PAIRS
                if p == 0:
                    pe.wait_ge(s_kmask, k + 1)
                    pe.wait_ge(s_qkch, 3 * k + 3)
                if g >= 2:
                    pe.wait_ge(s_shift, g - 1)
                nc.tensor.matmul(ps_s[g % 2][:], q_bd[:, k % 2, p, :],
                                 k_mask[:, k % 2, p].rearrange("q h j -> q (h j)"),
                                 start=True, stop=True).then_inc(s_scores, 1)

            def transpose_probs(g):
                pe.wait_ge(s_exp, g + 1)
                if g >= 1:
                    pe.wait_ge(s_ptsb, g)
                for hp in range(4):
                    ins = nc.tensor.transpose(ps_pt[:, hp * P:(hp + 1) * P],
                                              probs[:, g % 2, hp * P:(hp + 1) * P], ident)
                ins.then_inc(s_pt, 1)

            def weigh_values(g):
                k, p = g // PAIRS, g % PAIRS
                pe.wait_ge(s_ptsb, g + 1)
                if p == 0:
                    pe.wait_ge(s_vz, 2 * k + 2)
                    if k >= 2:
                        pe.wait_ge(s_attn, k - 1)
                for hp in range(4):
                    ins = nc.tensor.matmul(ps_u[k % 2][32 * hp:32 * hp + 32, p * P:(p + 1) * P],
                                           v_z[:, k % 2, p, 32 * hp:32 * hp + 32],
                                           probs_t[:, g % 2, hp * P:(hp + 1) * P],
                                           start=True, stop=True, tile_position=(0, 32 * hp))
                ins.then_inc(s_pv, 1)

            def x_transpose(k):
                pe.wait_ge(s_xhat, k + 1)
                if k >= 1:
                    pe.wait_ge(s_vz, 2 * k)
                for b in range(BLK):
                    ins = nc.tensor.transpose(ps_m0[:, b * P:(b + 1) * P],
                                              xhat[:, k % 2, b * P:(b + 1) * P], ident)
                ins.then_inc(s_x1, 1)

            def project_qk(k):
                pe.wait_ge(s_xn, k + 1)
                for i in range(2):
                    ins = nc.tensor.matmul(ps_m0[:, i * TOK:(i + 1) * TOK], w_qkv[:, i, :], xn[:, k % 2, :],
                                           start=True, stop=True)
                ins.then_inc(s_qk, 1)

            def project_v(k):
                pe.wait_ge(s_qkch, 3 * k + 3)
                nc.tensor.matmul(ps_m0[:, 0:TOK], w_qkv[:, 2, :], xn[:, k % 2, :],
                                 start=True, stop=True).then_inc(s_v, 1)

            def v_transpose(k):
                pe.wait_ge(s_vch, k + 1)
                if k == 0:
                    pe.wait_ge(s_late, 16)
                for p in range(PAIRS):
                    ins = nc.tensor.transpose(ps_m0[:, p * P:(p + 1) * P],
                                              v_ch[:, p].rearrange("q u j -> q (u j)"), perm_v)
                ins.then_inc(s_vt, 1)

            def recip_transpose(k):
                pe.wait_ge(s_recx, k + 1)
                if k >= 2:
                    pe.wait_ge(s_z, k - 1)
                for p in range(PAIRS):
                    ins = nc.tensor.transpose(
                        ps_m1[:, p * P:(p + 1) * P],
                        recip_x[:, p * HEADS:(p + 1) * HEADS, :].rearrange("q h e -> q (h e)"), ident)
                ins.then_inc(s_r, 1)

            def project_out(k):
                pe.wait_ge(s_attn, k + 1)
                if k == 0:
                    pe.wait_ge(s_latew, 4)
                if k >= 1:
                    pe.wait_ge(s_zhat, k)
                for w in range(2):
                    ins = nc.tensor.matmul(ps_m2[C * w:C * w + C, 0:TOK], w_out[:, w, :], attn[:, :, w, :],
                                           start=True, stop=True)
                ins.then_inc(s_proj, 1)

            def y_transpose(k):
                pe.wait_ge(s_y, k + 1)
                for b in range(BLK):
                    ins = nc.tensor.transpose(ps_m2[:, b * P:(b + 1) * P],
                                              y_tile[:, k % 2, b * P:(b + 1) * P], ident)
                ins.then_inc(s_yt, 1)

            def z_transpose(k):
                pe.wait_ge(s_zhat, k + 1)
                pe.wait_ge(s_rsb, min(k + 2, TILES))
                for b in range(BLK):
                    ins = nc.tensor.transpose(ps_m1[:, b * P:(b + 1) * P],
                                              zhat[:, k % 2, b * P:(b + 1) * P], ident)
                ins.then_inc(s_zt, 1)

            def fc1(s):
                pe.wait_ge(s_z, 2 * s + 2)
                for n in range(4):
                    w, m = n // M2, n % M2
                    if s >= 1:
                        pe.wait_ge(s_gelu, 4 * (s - 1) + n + 1)
                    nc.tensor.matmul(ps_h[n][:], w_fc1[:, w, m * P:(m + 1) * P],
                                     z_all[:, s * STEP:(s + 1) * STEP], start=True, stop=True).then_inc(s_fc1, 1)

            def fc2(s):
                if s >= 2:
                    pe.wait_ge(s_res, s - 1)
                for m in range(M2):
                    for w in range(2):
                        n = w * M2 + m
                        pe.wait_ge(s_gelu, 4 * s + n + 1)
                        ins = nc.tensor.matmul(ps_f[s % 2][C * w:C * w + C, :], w_fc2_t[:, m * C:(m + 1) * C],
                                               hidden[:, s % 2, n, :], start=(m == 0), stop=(m == M2 - 1))
                ins.then_inc(s_fc2, 1)

            pe.wait_ge(s_early, 16)
            for i in range(3):
                for w in range(2):
                    ins = nc.tensor.matmul(ps_u[1][C * w:C * w + C, i:i + 1], w_in_t[0:C, i * C:(i + 1) * C],
                                           vec[0:C, B1:B1 + 1], start=True, stop=True)
            ins.then_inc(s_bps, 1)
            x_transpose(0)
            pe.wait_ge(s_wqkv, 2)
            for t in range(-1, TILES):
                for p in range(PAIRS):
                    g = PAIRS * t + p
                    if g + 1 >= 0 and g + 1 < TILES * PAIRS and t >= 0:
                        scores(g + 1)
                    if p == 0 and tile_ok(t + 1):
                        project_qk(t + 1)
                    if p == 1:
                        if tile_ok(t - 1):
                            recip_transpose(t - 1)
                    if p == 2 and tile_ok(t - 2):
                        z_transpose(t - 2)
                    if t >= 0:
                        transpose_probs(g)
                        if g >= 1:
                            weigh_values(g - 1)
                    if p == 1 and tile_ok(t + 1):
                        project_v(t + 1)
                    if p == 2:
                        if tile_ok(t + 1):
                            v_transpose(t + 1)
                        if tile_ok(t - 1):
                            project_out(t - 1)
                    if p == 3:
                        if tile_ok(t + 2):
                            x_transpose(t + 2)
                        if tile_ok(t - 1):
                            y_transpose(t - 1)
                    if t == -1 and p == 3:
                        pe.wait_ge(s_late, 16)
                        pe.wait_ge(s_bias, 2)
                        nc.tensor.matmul(ps_u[1][:, 0:C], out_w_x, proj_w_t[:, 0:C], start=True, stop=True)
                        nc.tensor.matmul(ps_u[1][:, C:C + 1], proj_w_t, vec[0:C, OUTB:OUTB + 1],
                                         start=True, stop=True)
                        for m in range(M2):
                            ins = nc.tensor.matmul(ps_u[1][:, C + 1 + m:C + 2 + m],
                                                   w_fc1_t[0:C, m * P:(m + 1) * P],
                                                   vec[0:C, B2:B2 + 1], start=True, stop=True)
                        ins.then_inc(s_lps, 1)
                        scores(0)
            weigh_values(TILES * PAIRS - 1)
            fc1(0)
            recip_transpose(TILES - 1)
            z_transpose(TILES - 2)
            fc2(0)
            project_out(TILES - 1)
            fc1(1)
            y_transpose(TILES - 1)
            fc2(1)
            fc1(2)
            z_transpose(TILES - 1)
            fc2(2)
            fc1(3)
            fc2(3)

        @block.vector
        def _(dve):
            def stats(k, src, stats_b, mv_b, s_st, s_mv):
                for n in range(GRP):
                    ins = nc.vector.bn_stats(stats_b[:, k % 2, n, :], src[:, n * C:(n + 1) * C])
                ins.then_inc(s_st, 1)
                dve.wait_ge(s_st, k + 1)
                for n in range(GRP):
                    ins = nc.vector.bn_aggr(mv_b[:, k % 2, n, :], stats_b[:, k % 2, n, :])
                ins.then_inc(s_mv, 1)

            def normalise(k, dst, src, mv_b, rstd_b, s_done):
                for n in range(GRP):
                    ins = nc.vector.tensor_scalar(dst[:, k % 2, n * C:(n + 1) * C], src[:, n * C:(n + 1) * C],
                                                  mv_b[:, k % 2, n, 0:1], rstd_b[:, k % 2, n:n + 1],
                                                  op0=ALU.subtract, op1=ALU.mult)
                ins.then_inc(s_done, 1)

            def ln1_stats(k):
                dve.wait_ge(s_xtok[xtok_load(k)], 16)
                if k >= 2:
                    dve.wait_ge(s_var1, k - 1)
                stats(k, x_tok[:, k * TOK:(k + 1) * TOK], stats1, mv1, s_st1, s_mv1)

            def ln1_apply(k):
                dve.wait_ge(s_rstd1, k + 1)
                if k >= 2:
                    dve.wait_ge(s_x1, k - 1)
                normalise(k, xhat, x_tok[:, k * TOK:(k + 1) * TOK], mv1, rstd1, s_xhat)

            def ln2_stats(k):
                dve.wait_ge(s_yt, k + 1)
                stats(k, ps_m2[:, 0:TOK], stats2, mv2, s_st2, s_mv2)

            def ln2_apply(k):
                dve.wait_ge(s_rstd2, k + 1)
                if k >= 2:
                    dve.wait_ge(s_zt, k - 1)
                normalise(k, zhat, ps_m2[:, 0:TOK], mv2, rstd2, s_zhat)

            def softmax_shift(g):
                s3 = ps_s[g % 2][:].rearrange("q (h j) -> q h j", h=HEADS)
                dve.wait_ge(s_scores, g + 1)
                nc.vector.tensor_reduce(row_max[:, g % 2, :], s3, axis=AX.X, op=ALU.max).then_inc(s_max, 1)
                dve.wait_ge(s_max, g + 1)
                if g >= 2:
                    dve.wait_ge(s_exp, g - 1)
                nc.vector.tensor_tensor(shifted[:, g % 2, :].rearrange("q (h j) -> q h j", h=HEADS), s3,
                                        row_max[:, g % 2, :].unsqueeze(2).to_broadcast([P, HEADS, L]),
                                        op=ALU.subtract).then_inc(s_shift, 1)

            def softmax_sum(g):
                k, p = g // PAIRS, g % PAIRS
                dve.wait_ge(s_exp, g + 1)
                nc.vector.tensor_reduce(row_sum[:, k % 2, p, :],
                                        probs[:, g % 2, :].rearrange("q (h j) -> q h j", h=HEADS),
                                        axis=AX.X, op=ALU.add).then_inc(s_sum, 1)

            def reciprocal(k):
                dve.wait_ge(s_sum, PAIRS * (k + 1))
                if k >= 1:
                    dve.wait_ge(s_recx, k)
                nc.vector.reciprocal(recip[:], row_sum[:, k % 2].rearrange("q p h -> q (p h)")).then_inc(s_recip, 1)

            def normalise_attn(k):
                dve.wait_ge(s_pv, PAIRS * (k + 1))
                dve.wait_ge(s_rsb, k + 1)
                if k >= 1:
                    dve.wait_ge(s_proj, k)
                nc.vector.tensor_tensor(attn[:].rearrange("q p w i -> q (p w i)"), ps_u[k % 2][:], recip_t[:],
                                        op=ALU.mult).then_inc(s_attn, 1)

            def residual(k):
                dve.wait_ge(s_proj, k + 1)
                if k == 0:
                    dve.wait_ge(s_xch, 16)
                if k >= 2:
                    dve.wait_ge(s_yt, k - 1)
                    dve.wait_ge(s_ycopy, k - 1)
                nc.vector.scalar_tensor_tensor(y_tile[:, k % 2, :], ps_m2[:, 0:TOK], b_out[:, 0:1],
                                               x_ch[:, k * TOK:(k + 1) * TOK],
                                               op0=ALU.add, op1=ALU.add).then_inc(s_y, 1)

            def finish(s):
                dve.wait_ge(s_fc2, s + 1)
                if s >= 2:
                    dve.wait_ge(s_out[s - 2], 16)
                nc.vector.scalar_tensor_tensor(result[:, s % 2, :], ps_f[s % 2][:], vec[:, FC2B:FC2B + 1],
                                               y_all[:, s * STEP:(s + 1) * STEP],
                                               op0=ALU.add, op1=ALU.add).then_inc(s_res, 1)

            ln1_stats(0)
            dve.wait_ge(s_early, 16)
            for w in range(2):
                nc.vector.tensor_scalar(w_qkv[:, :, w * C:(w + 1) * C],
                                        w_in_t.rearrange("q (s e) -> q s e", s=3),
                                        vec[:, G1:G1 + 1], half_mask[:, w:w + 1],
                                        op0=ALU.mult, op1=ALU.mult).then_inc(s_wqkv, 1)
            ln1_apply(0)
            dve.wait_ge(s_bps, 1)
            nc.vector.tensor_tensor(b_qkv[:, 0:3], ps_u[1][:, 0:3], vec[:, BQ:BQ + 3], op=ALU.add).then_inc(s_bias, 1)
            dve.wait_ge(s_bias, 1)
            nc.vector.tensor_scalar(b_qkv[:, 3:4], b_qkv[:, 0:1], float(D) ** -0.5, None,
                                    op0=ALU.mult).then_inc(s_bias, 1)
            ln1_stats(1)
            ln1_apply(1)
            dve.wait_ge(s_late, 16)
            for w in range(2):
                nc.vector.tensor_scalar(w_fc1[:, w, :], w_fc1_t, vec[:, G2:G2 + 1], half_mask[:, w:w + 1],
                                        op0=ALU.mult, op1=ALU.mult).then_inc(s_latew, 1)
            dve.wait_ge(s_lps, 1)
            for w in range(2):
                nc.vector.tensor_scalar(w_out[:, w, :], ps_u[1][:, 0:C], row_mask[:, w:w + 1], None,
                                        op0=ALU.mult).then_inc(s_latew, 1)
            nc.vector.tensor_tensor(b_out[:], ps_u[1][:, C:C + 1], vec[:, PROJB:PROJB + 1],
                                    op=ALU.add).then_inc(s_latew, 1)
            nc.vector.tensor_tensor(b_fc1[:], ps_u[1][:, C + 1:C + 1 + M2], vec[:, FC1B:FC1B + M2],
                                    op=ALU.add).then_inc(s_latew, 1)
            softmax_shift(0)
            for t in range(TILES):
                for p in range(PAIRS):
                    g = PAIRS * t + p
                    if g + 1 < TILES * PAIRS:
                        softmax_shift(g + 1)
                    softmax_sum(g)
                    if p == 0:
                        if tile_ok(t - 2):
                            ln2_stats(t - 2)
                    if p == 1:
                        if tile_ok(t - 2):
                            ln2_apply(t - 2)
                        if tile_ok(t - 1):
                            normalise_attn(t - 1)
                    if p == 2:
                        if tile_ok(t + 2):
                            ln1_stats(t + 2)
                            ln1_apply(t + 2)
                        if tile_ok(t - 1):
                            residual(t - 1)
                    if p == 3:
                        reciprocal(t)
            ln2_stats(TILES - 2)
            normalise_attn(TILES - 1)
            ln2_apply(TILES - 2)
            residual(TILES - 1)
            finish(0)
            ln2_stats(TILES - 1)
            ln2_apply(TILES - 1)
            for s in range(1, STEPS):
                finish(s)

        @block.scalar
        def _(act):
            def evacuate_xn(k):
                act.wait_ge(s_x1, k + 1)
                nc.scalar.activation(xn[:, k % 2, :], ps_m0[:, 0:TOK], ACT.Copy).then_inc(s_xn, 1)

            def evacuate_qk(k):
                act.wait_ge(s_qk, k + 1)
                for w in range(2):
                    r = slice(C * w, C * w + C)
                    nc.scalar.activation(q_bd[r, k % 2, :, w * L:(w + 1) * L],
                                         ps_m0[r, 0:TOK].rearrange("q (p i) -> q p i", p=PAIRS),
                                         ACT.Identity, bias=b_qkv[r, 3:4], scale=float(D) ** -0.5).then_inc(s_qkch, 1)
                nc.scalar.activation(k_ch[:, k % 2, :], ps_m0[:, TOK:2 * TOK], ACT.Identity,
                                     bias=b_qkv[:, 1:2]).then_inc(s_qkch, 1)

            def evacuate_v(k):
                act.wait_ge(s_v, k + 1)
                nc.scalar.activation(v_ch[:], ps_m0[:, 0:TOK].rearrange("q (p i) -> q p i", p=PAIRS)
                                     .unsqueeze(2).to_broadcast([P, PAIRS, 2, L]),
                                     ACT.Identity, bias=b_qkv[:, 2:3]).then_inc(s_vch, 1)

            def evacuate_vt(k):
                act.wait_ge(s_vt, k + 1)
                for u in range(2):
                    r = slice(L * u, L * u + L)
                    c = slice(2 * D * u, 2 * D * u + 2 * D)
                    nc.scalar.activation(
                        v_z[r, k % 2].rearrange("q p (a e) -> q (p a) e", e=4 * D)[:, :, c],
                        ps_m0[r, :].rearrange("q (b e) -> q b e", e=4 * D)[:, :, c],
                        ACT.Copy).then_inc(s_vz, 1)

            def exponentiate(g):
                act.wait_ge(s_shift, g + 1)
                if g >= 2:
                    act.wait_ge(s_pt, g - 1)
                    act.wait_ge(s_sum, g - 1)
                nc.scalar.activation(probs[:, g % 2, :], shifted[:, g % 2, :], ACT.Exp).then_inc(s_exp, 1)

            def evacuate_pt(g):
                act.wait_ge(s_pt, g + 1)
                if g >= 2:
                    act.wait_ge(s_pv, g - 1)
                nc.scalar.activation(probs_t[:, g % 2, :], ps_pt[:], ACT.Copy).then_inc(s_ptsb, 1)

            def evacuate_r(k):
                act.wait_ge(s_r, k + 1)
                if k >= 1:
                    act.wait_ge(s_attn, k)
                nc.scalar.activation(recip_t[:], ps_m1[:], ACT.Copy).then_inc(s_rsb, 1)

            def evacuate_z(k):
                act.wait_ge(s_zt, k + 1)
                nc.scalar.activation(z_all[:, k * TOK:(k + 1) * TOK], ps_m1[:, 0:TOK], ACT.Copy).then_inc(s_z, 1)

            def gelu(s):
                for n in range(4):
                    act.wait_ge(s_fc1, 4 * s + n + 1)
                    if s >= 2:
                        act.wait_ge(s_fc2, s - 1)
                    nc.scalar.activation(hidden[:, s % 2, n, :], ps_h[n][:], ACT.Gelu,
                                         bias=b_fc1[:, n % M2:n % M2 + 1]).then_inc(s_gelu, 1)

            act.dma_start(early[:], early_d).then_inc(s_early, 16)
            evacuate_xn(0)
            act.wait_ge(s_bias, 2)
            act.wait_ge(s_zero, 3)
            evacuate_qk(0)
            evacuate_v(0)
            evacuate_vt(0)
            evacuate_xn(1)
            exponentiate(0)
            for t in range(TILES):
                for p in range(PAIRS):
                    g = PAIRS * t + p
                    if g + 1 < TILES * PAIRS:
                        exponentiate(g + 1)
                    evacuate_pt(g)
                    if p == 0 and tile_ok(t + 1):
                        evacuate_qk(t + 1)
                    if p == 1:
                        if tile_ok(t - 1):
                            evacuate_r(t - 1)
                        if tile_ok(t + 1):
                            evacuate_v(t + 1)
                    if p == 2:
                        if tile_ok(t - 2):
                            evacuate_z(t - 2)
                        if tile_ok(t + 1):
                            evacuate_vt(t + 1)
                    if p == 3 and tile_ok(t + 2):
                        evacuate_xn(t + 2)
            act.wait_ge(s_latew, 6)
            evacuate_r(TILES - 1)
            gelu(0)
            evacuate_z(TILES - 2)
            gelu(1)
            gelu(2)
            evacuate_z(TILES - 1)
            gelu(3)

        @block.gpsimd
        def _(pool):
            def rstd(k, mv_b, var_b, rstd_b, s_mv, s_var, s_rstd):
                pool.wait_ge(s_mv, k + 1)
                nc.gpsimd.tensor_scalar(var_b[:, k % 2, :], mv_b[:, k % 2, :, 1], 1.0, EPS,
                                        op0=ALU.mult, op1=ALU.add).then_inc(s_var, 1)
                pool.wait_ge(s_var, k + 1)
                nc.gpsimd.tensor_tensor(rstd_b[:, k % 2, :], var_b[:, k % 2, :], minus_half[:],
                                        op=ALU.pow).then_inc(s_rstd, 1)

            def mask_k(k):
                pool.wait_ge(s_qkch, 3 * k + 3)
                if k == 0:
                    pool.wait_ge(s_early, 16)
                for h in range(HEADS):
                    ins = nc.gpsimd.tensor_scalar(k_mask[:, k % 2, :, h, :],
                                                  k_ch[:, k % 2, :].rearrange("q (p j) -> q p j", p=PAIRS),
                                                  head_mask[:, h:h + 1], 0.0, op0=ALU.mult, op1=ALU.add)
                ins.then_inc(s_kmask, 1)

            def expand_recip(k):
                pool.wait_ge(s_recip, k + 1)
                if k >= 1:
                    pool.wait_ge(s_r, k)
                nc.gpsimd.tensor_scalar(recip_x[:], recip[:].unsqueeze(2).to_broadcast([P, PAIRS * HEADS, 2 * D]),
                                        1.0, 0.0, op0=ALU.mult, op1=ALU.add).then_inc(s_recx, 1)

            def copy_y(k):
                pool.wait_ge(s_y, k + 1)
                nc.gpsimd.tensor_scalar(y_all[:, k * TOK:(k + 1) * TOK], y_tile[:, k % 2, :], 1.0, 0.0,
                                        op0=ALU.mult, op1=ALU.add).then_inc(s_ycopy, 1)

            nc.gpsimd.memset(minus_half[:], -0.5).then_inc(s_zero, 1)
            nc.gpsimd.memset(q_bd[:], 0.0).then_inc(s_zero, 1)
            nc.gpsimd.memset(v_z[:], 0.0).then_inc(s_zero, 1)
            pool.wait_ge(s_zero, 1)
            rstd(0, mv1, var1, rstd1, s_mv1, s_var1, s_rstd1)
            rstd(1, mv1, var1, rstd1, s_mv1, s_var1, s_rstd1)
            mask_k(0)
            for t in range(TILES + 1):
                if tile_ok(t - 1):
                    expand_recip(t - 1)
                if tile_ok(t - 2):
                    rstd(t - 2, mv2, var2, rstd2, s_mv2, s_var2, s_rstd2)
                if tile_ok(t + 1):
                    mask_k(t + 1)
                if tile_ok(t + 2):
                    rstd(t + 2, mv1, var1, rstd1, s_mv1, s_var1, s_rstd1)
                if tile_ok(t - 1):
                    copy_y(t - 1)
            rstd(TILES - 1, mv2, var2, rstd2, s_mv2, s_var2, s_rstd2)


def kernel(**inputs):
    import concourse.bacc as bacc
    from concourse.bass_utils import run_bass_kernel_spmd

    a = {k.replace("L0_conv_", ""): np.asarray(v) for k, v in inputs.items()}
    f = a["x"].dtype
    xr = np.roll(a["x"], (-SHIFT, -SHIFT), (2, 3)).reshape(2, TILES, C, HH // WIN, WIN, WW // WIN, WIN)
    x_ch = xr.transpose(0, 2, 1, 3, 5, 4, 6).reshape(P, ALL)
    x_tok = xr.transpose(5, 4, 6, 1, 3, 0, 2).reshape(P, ALL)

    q = np.arange(P)
    ident = np.eye(P, dtype=f)
    masks = np.zeros((P, NM), f)
    masks[q, q // C] = 1
    masks[q, 2 + q % C // D] = 1
    masks[q, 10 + q // D % 2] = 1
    perm = ident.reshape(P, 2, HEADS, D).transpose(0, 2, 1, 3).reshape(P, P)

    def twice(v):
        return np.concatenate([v, v], 0)

    in_b = a["in_b"].reshape(3, C)
    vecs = np.stack([twice(a["norm1_g"]), twice(a["norm1_b"]), twice(in_b[0]), twice(in_b[1]), twice(in_b[2]),
                     twice(a["out_b"]), twice(a["proj_b"]), twice(a["norm2_g"]), twice(a["norm2_b"]),
                     twice(a["fc2_b"]), a["fc1_b"][:P], a["fc1_b"][P:]], 1)
    early = np.concatenate([ident, masks, vecs, twice(a["in_w"].T)], 1)
    out_w_x = a["out_w"].reshape(C, HEADS, 1, D).repeat(2, 2).reshape(C, P)
    proj_w_t = np.concatenate([a["proj_w"].T, a["proj_w"].T], 1)
    late = np.concatenate([perm, twice(a["fc1_w"].T),
                           a["fc2_w"].T.reshape(M2, P, C).transpose(1, 0, 2).reshape(P, M2 * C),
                           twice(out_w_x), twice(proj_w_t)], 1)

    nc = bacc.Bacc("TRN2", target_bir_lowering=False, num_devices=1)
    arrays, args = {}, []
    for name, v in (("x_tok_d", x_tok), ("x_ch_d", x_ch), ("early_d", early), ("late_d", late)):
        arrays[name] = np.ascontiguousarray(v)
        args.append(nc.dram_tensor(name, v.shape, mybir.dt.from_np(v.dtype), kind="ExternalInput").ap())
    args.append(nc.dram_tensor("out_d", (P, ALL), F32, kind="ExternalOutput").ap())
    swin_block_kernel(nc, *args)
    r = run_bass_kernel_spmd(nc, [arrays], core_ids=[0])
    out = np.asarray(r.results[0]["out_d"]).reshape(2, C, TILES, HH // WIN, WW // WIN, WIN, WIN)
    out = out.transpose(0, 2, 1, 3, 5, 4, 6).reshape(B, C, HH, WW)
    return np.roll(out, (SHIFT, SHIFT), (2, 3))
```

```python
from contextlib import ExitStack

import numpy as np

import concourse.bass as bass
from concourse import mybir

F32 = mybir.dt.float32
F32R = mybir.dt.float32r
ALU = mybir.AluOpType
ACT = mybir.ActivationFunctionType
AX = mybir.AxisListType

B, C, HH, WW = 16, 64, 16, 16
WIN, SHIFT = 8, 4
HEADS = 8
D = C // HEADS
HIDDEN = 4 * C
EPS = 1e-6
P = 128
TOK = HH * WW
TILES = B // 2
L = WIN * WIN
PAIRS = TOK // L
BLK = TOK // P
GRP = BLK * 2
M2 = HIDDEN // P
STEP = 2 * TOK
STEPS = TILES // 2
ALL = TILES * TOK
NV = 12
G1, B1, BQ, OUTB, PROJB, G2, B2, FC2B, FC1B = 0, 1, 2, 5, 6, 7, 8, 9, 10
NM = 12
EARLY = P + NM + NV + 3 * C
LATE = P + HIDDEN + M2 * C + 2 * P


def swin_block_kernel(nc, x_tok_d, x_ch_d, early_d, late_d, out_d):
    ctx = ExitStack()
    with ctx:
        def sb(name, shape, dtype=F32):
            return ctx.enter_context(nc.sbuf_tensor(name, shape, dtype))

        def bank(name):
            return ctx.enter_context(nc.psum_tensor(name, [P, 512], F32))

        def sem(name):
            return ctx.enter_context(nc.semaphore(name))

        x_tok = sb("x_tok", [P, ALL])
        x_ch = sb("x_ch", [P, ALL])
        early = sb("early", [P, EARLY])
        late = sb("late", [P, LATE])
        ident = early[:, 0:P]
        half_mask = early[:, P:P + 2]
        head_mask = early[:, P + 2:P + 2 + HEADS]
        row_mask = early[:, P + 10:P + 12]
        vec = early[:, P + NM:P + NM + NV]
        w_in_t = early[:, P + NM + NV:EARLY]
        perm_v = late[:, 0:P]
        w_fc1_t = late[:, P:P + HIDDEN]
        w_fc2_t = late[:, P + HIDDEN:P + HIDDEN + M2 * C]
        out_w_x = late[0:C, LATE - 2 * P:LATE - P]
        proj_w_t = late[0:C, LATE - P:LATE]

        w_qkv = sb("w_qkv", [P, 3, P])
        b_qkv = sb("b_qkv", [P, 4])
        w_out = sb("w_out", [P, 2, C])
        b_out = sb("b_out", [P, 1])
        w_fc1 = sb("w_fc1", [P, 2, HIDDEN])
        b_fc1 = sb("b_fc1", [P, M2])

        stats1 = sb("stats1", [P, 2, GRP, 6])
        mv1 = sb("mv1", [P, 2, GRP, 2])
        var1 = sb("var1", [P, 2, GRP])
        rstd1 = sb("rstd1", [P, 2, GRP])
        stats2 = sb("stats2", [P, 2, GRP, 6])
        mv2 = sb("mv2", [P, 2, GRP, 2])
        var2 = sb("var2", [P, 2, GRP])
        rstd2 = sb("rstd2", [P, 2, GRP])
        minus_half = sb("minus_half", [P, GRP])
        xhat = sb("xhat", [P, 2, TOK])
        zhat = sb("zhat", [P, 2, TOK])

        xn = sb("xn", [P, 2, TOK])
        q_bd = sb("q_bd", [P, 2, PAIRS, P])
        k_ch = sb("k_ch", [P, 2, TOK])
        k_mask = sb("k_mask", [P, 2, PAIRS, HEADS, L])
        v_ch = sb("v_ch", [P, PAIRS, 2, L])
        v_z = sb("v_z", [P, 2, PAIRS, P])
        row_max = sb("row_max", [P, 2, HEADS], F32R)
        minus_ident = sb("minus_ident", [P, P], F32R)
        probs = sb("probs", [P, 2, 512])
        probs_t = sb("probs_t", [P, 2, 512])
        row_sum = sb("row_sum", [P, 2, PAIRS, HEADS])
        recip = sb("recip", [P, PAIRS * HEADS])
        recip_x = sb("recip_x", [P, PAIRS * HEADS, 2 * D])
        recip_t = sb("recip_t", [P, 512])
        attn = sb("attn", [P, PAIRS, 2, L])
        y_tile = sb("y_tile", [P, 2, TOK])
        y_all = sb("y_all", [P, ALL])
        z_all = sb("z_all", [P, ALL])

        hidden = sb("hidden", [P, 2, 4, STEP])
        result = sb("result", [P, 2, STEP])

        ps_s = [bank("ps_s0"), bank("ps_s1")]
        ps_pt = bank("ps_pt")
        ps_u = [bank("ps_u0"), bank("ps_u1")]
        ps_m0, ps_m1, ps_m2 = bank("ps_m0"), bank("ps_m1"), bank("ps_m2")
        ps_h = [ps_s[0], ps_s[1], ps_pt, ps_m0]
        ps_f = ps_u

        s_early, s_late = sem("s_early"), sem("s_late")
        s_xtok, s_xch = [sem(f"s_xtok{i}") for i in range(4)], sem("s_xch")
        s_ident = sem("s_ident")
        s_zero, s_wqkv, s_bps, s_bias, s_lps, s_latew = (
            sem("s_zero"), sem("s_wqkv"), sem("s_bps"), sem("s_bias"), sem("s_lps"), sem("s_latew"))
        s_st1, s_mv1, s_var1, s_rstd1, s_xhat, s_x1, s_xn = (
            sem("s_st1"), sem("s_mv1"), sem("s_var1"), sem("s_rstd1"), sem("s_xhat"), sem("s_x1"), sem("s_xn"))
        s_qk, s_qkch, s_kmask, s_v, s_vch, s_vt, s_vz = (
            sem("s_qk"), sem("s_qkch"), sem("s_kmask"), sem("s_v"), sem("s_vch"), sem("s_vt"), sem("s_vz"))
        s_scores, s_max, s_shifted, s_exp, s_sum, s_pt, s_ptsb, s_pv = (
            sem("s_scores"), sem("s_max"), sem("s_shifted"), sem("s_exp"), sem("s_sum"), sem("s_pt"),
            sem("s_ptsb"), sem("s_pv"))
        s_recip, s_recx, s_r, s_rsb, s_attn, s_proj, s_y, s_ycopy, s_yt = (
            sem("s_recip"), sem("s_recx"), sem("s_r"), sem("s_rsb"), sem("s_attn"), sem("s_proj"),
            sem("s_y"), sem("s_ycopy"), sem("s_yt"))
        s_st2, s_mv2, s_var2, s_rstd2, s_zhat, s_zt, s_z = (
            sem("s_st2"), sem("s_mv2"), sem("s_var2"), sem("s_rstd2"), sem("s_zhat"), sem("s_zt"), sem("s_z"))
        s_fc1, s_gelu, s_fc2, s_res = sem("s_fc1"), sem("s_gelu"), sem("s_fc2"), sem("s_res")
        s_out = [sem(f"s_out{s}") for s in range(STEPS)]

        XTOK = [(0, 1), (1, 2), (2, 4), (4, 8)]

        def xtok_load(k):
            return next(i for i, (a, b) in enumerate(XTOK) if a <= k < b)

        def tile_ok(k):
            return not isinstance(k, int) or 0 <= k < TILES

        def later(k, n):
            return not isinstance(k, int) or k >= n

        def all_tiles(eng, first, tile):
            for t in range(first, TILES):
                tile(t, t % 2)

        block = ctx.enter_context(nc.Block())

        @block.sync
        def _(sp):
            a, b = XTOK[0]
            sp.dma_start(x_tok[:, a * TOK:b * TOK], x_tok_d[:, a * TOK:b * TOK]).then_inc(s_xtok[0], 16)
            for i in range(1, 4):
                a, b = XTOK[i]
                sp.dma_start(x_tok[:, a * TOK:b * TOK], x_tok_d[:, a * TOK:b * TOK]).then_inc(s_xtok[i], 16)
            sp.dma_start(late[:], late_d).then_inc(s_late, 16)
            sp.dma_start(x_ch[:], x_ch_d).then_inc(s_xch, 16)
            for s in range(STEPS):
                sp.wait_ge(s_res, s + 1)
                sp.dma_start(out_d[:, s * STEP:(s + 1) * STEP], result[:, s % 2, :]).then_inc(s_out[s], 16)
            for s in range(STEPS):
                sp.wait_ge(s_out[s], 16)

        @block.tensor
        def _(pe):
            def scores(k, b, p):
                if p == 0:
                    pe.wait_ge(s_kmask, k + 1)
                    pe.wait_ge(s_qkch, 3 * k + 3)
                if later(k * PAIRS + p, 2):
                    pe.wait_ge(s_exp, k * PAIRS + p - 1)
                nc.tensor.matmul(ps_s[p % 2][:], q_bd[:, b, p, :],
                                 k_mask[:, b, p].rearrange("q h j -> q (h j)"),
                                 start=True, stop=True).then_inc(s_scores, 1)

            def shift_scores(k, b, p):
                if not later(k * PAIRS + p, 1):
                    pe.wait_ge(s_ident, 1)
                pe.wait_ge(s_max, k * PAIRS + p + 1)
                nc.tensor.matmul(ps_s[p % 2][:], minus_ident[:],
                                 row_max[:, p % 2, :].unsqueeze(2).to_broadcast([P, HEADS, L]),
                                 start=False, stop=True, skip_group_check=True).then_inc(s_shifted, 1)

            def transpose_probs(k, b, p):
                pe.wait_ge(s_exp, k * PAIRS + p + 1)
                if later(k * PAIRS + p, 1):
                    pe.wait_ge(s_ptsb, k * PAIRS + p)
                for hp in range(4):
                    ins = nc.tensor.transpose(ps_pt[:, hp * P:(hp + 1) * P],
                                              probs[:, p % 2, hp * P:(hp + 1) * P], ident)
                ins.then_inc(s_pt, 1)

            def weigh_values(k, b, p):
                pe.wait_ge(s_ptsb, k * PAIRS + p + 1)
                if p == 0:
                    pe.wait_ge(s_vz, 2 * k + 2)
                    if later(k, 2):
                        pe.wait_ge(s_attn, k - 1)
                for hp in range(4):
                    ins = nc.tensor.matmul(ps_u[b][32 * hp:32 * hp + 32, p * P:(p + 1) * P],
                                           v_z[:, b, p, 32 * hp:32 * hp + 32],
                                           probs_t[:, p % 2, hp * P:(hp + 1) * P],
                                           start=True, stop=True, tile_position=(0, 32 * hp))
                ins.then_inc(s_pv, 1)

            def x_transpose(k, b):
                pe.wait_ge(s_xhat, k + 1)
                if later(k, 1):
                    pe.wait_ge(s_vz, 2 * k)
                for n in range(BLK):
                    ins = nc.tensor.transpose(ps_m0[:, n * P:(n + 1) * P],
                                              xhat[:, b, n * P:(n + 1) * P], ident)
                ins.then_inc(s_x1, 1)

            def project_qk(k, b):
                pe.wait_ge(s_xn, k + 1)
                for i in range(2):
                    ins = nc.tensor.matmul(ps_m0[:, i * TOK:(i + 1) * TOK], w_qkv[:, i, :], xn[:, b, :],
                                           start=True, stop=True)
                ins.then_inc(s_qk, 1)

            def project_v(k, b):
                pe.wait_ge(s_qkch, 3 * k + 3)
                nc.tensor.matmul(ps_m0[:, 0:TOK], w_qkv[:, 2, :], xn[:, b, :],
                                 start=True, stop=True).then_inc(s_v, 1)

            def v_transpose(k, b):
                pe.wait_ge(s_vch, k + 1)
                if not later(k, 1):
                    pe.wait_ge(s_late, 16)
                for p in range(PAIRS):
                    ins = nc.tensor.transpose(ps_m0[:, p * P:(p + 1) * P],
                                              v_ch[:, p].rearrange("q u j -> q (u j)"), perm_v)
                ins.then_inc(s_vt, 1)

            def recip_transpose(k, b):
                pe.wait_ge(s_recx, k + 1)
                if later(k, 2):
                    pe.wait_ge(s_z, k - 1)
                for p in range(PAIRS):
                    ins = nc.tensor.transpose(
                        ps_m1[:, p * P:(p + 1) * P],
                        recip_x[:, p * HEADS:(p + 1) * HEADS, :].rearrange("q h e -> q (h e)"), ident)
                ins.then_inc(s_r, 1)

            def project_out(k, b):
                pe.wait_ge(s_attn, k + 1)
                if not later(k, 1):
                    pe.wait_ge(s_latew, 4)
                if later(k, 1):
                    pe.wait_ge(s_zhat, k)
                for w in range(2):
                    ins = nc.tensor.matmul(ps_m2[C * w:C * w + C, 0:TOK], w_out[:, w, :], attn[:, :, w, :],
                                           start=True, stop=True)
                ins.then_inc(s_proj, 1)

            def y_transpose(k, b):
                pe.wait_ge(s_y, k + 1)
                for n in range(BLK):
                    ins = nc.tensor.transpose(ps_m2[:, n * P:(n + 1) * P],
                                              y_tile[:, b, n * P:(n + 1) * P], ident)
                ins.then_inc(s_yt, 1)

            def z_transpose(k, b):
                pe.wait_ge(s_zhat, k + 1)
                pe.wait_ge(s_rsb, k + 1 + tile_ok(k + 1))
                for n in range(BLK):
                    ins = nc.tensor.transpose(ps_m1[:, n * P:(n + 1) * P],
                                              zhat[:, b, n * P:(n + 1) * P], ident)
                ins.then_inc(s_zt, 1)

            def fc1(s):
                pe.wait_ge(s_z, 2 * s + 2)
                for n in range(4):
                    w, m = n // M2, n % M2
                    if s >= 1:
                        pe.wait_ge(s_gelu, 4 * (s - 1) + n + 1)
                    nc.tensor.matmul(ps_h[n][:], w_fc1[:, w, m * P:(m + 1) * P],
                                     z_all[:, s * STEP:(s + 1) * STEP], start=True, stop=True).then_inc(s_fc1, 1)

            def fc2(s):
                if s >= 2:
                    pe.wait_ge(s_res, s - 1)
                for m in range(M2):
                    for w in range(2):
                        n = w * M2 + m
                        pe.wait_ge(s_gelu, 4 * s + n + 1)
                        ins = nc.tensor.matmul(ps_f[s % 2][C * w:C * w + C, :], w_fc2_t[:, m * C:(m + 1) * C],
                                               hidden[:, s % 2, n, :], start=(m == 0), stop=(m == M2 - 1))
                ins.then_inc(s_fc2, 1)

            def tile(t, b):
                last = isinstance(t, int) and t == TILES - 1
                for p in range(PAIRS):
                    nk, nb, np_ = (t, b, p + 1) if p + 1 < PAIRS else (t + 1, 1 - b, 0)
                    more = not (last and p == PAIRS - 1)
                    if more:
                        scores(nk, nb, np_)
                    transpose_probs(t, b, p)
                    if p >= 1:
                        weigh_values(t, b, p - 1)
                    elif tile_ok(t - 1):
                        weigh_values(t - 1, 1 - b, PAIRS - 1)
                    if p == 0:
                        if tile_ok(t + 1):
                            project_qk(t + 1, 1 - b)
                        if tile_ok(t - 1):
                            recip_transpose(t - 1, 1 - b)
                    if p == 1 and tile_ok(t + 1):
                        project_v(t + 1, 1 - b)
                    if p == 2:
                        if tile_ok(t + 1):
                            v_transpose(t + 1, 1 - b)
                        if tile_ok(t - 1):
                            project_out(t - 1, 1 - b)
                    if p == 3:
                        if tile_ok(t - 2):
                            z_transpose(t - 2, b)
                        if tile_ok(t + 2):
                            x_transpose(t + 2, b)
                        if tile_ok(t - 1):
                            y_transpose(t - 1, 1 - b)
                    if more:
                        shift_scores(nk, nb, np_)

            pe.wait_ge(s_early, 16)
            for i in range(3):
                for w in range(2):
                    ins = nc.tensor.matmul(ps_u[1][C * w:C * w + C, i:i + 1], w_in_t[0:C, i * C:(i + 1) * C],
                                           vec[0:C, B1:B1 + 1], start=True, stop=True)
            ins.then_inc(s_bps, 1)
            x_transpose(0, 0)
            pe.wait_ge(s_wqkv, 2)
            project_qk(0, 0)
            project_v(0, 0)
            pe.wait_ge(s_late, 16)
            pe.wait_ge(s_bias, 2)
            nc.tensor.matmul(ps_u[1][:, 0:C], out_w_x, proj_w_t[:, 0:C], start=True, stop=True)
            nc.tensor.matmul(ps_u[1][:, C:C + 1], proj_w_t, vec[0:C, OUTB:OUTB + 1],
                             start=True, stop=True)
            for m in range(M2):
                ins = nc.tensor.matmul(ps_u[1][:, C + 1 + m:C + 2 + m], w_fc1_t[0:C, m * P:(m + 1) * P],
                                       vec[0:C, B2:B2 + 1], start=True, stop=True)
            ins.then_inc(s_lps, 1)
            v_transpose(0, 0)
            scores(0, 0, 0)
            shift_scores(0, 0, 0)
            x_transpose(1, 1)
            all_tiles(pe, 0, tile)
            weigh_values(TILES - 1, 1, PAIRS - 1)
            fc1(0)
            recip_transpose(TILES - 1, 1)
            z_transpose(TILES - 2, 0)
            fc2(0)
            project_out(TILES - 1, 1)
            fc1(1)
            y_transpose(TILES - 1, 1)
            fc2(1)
            fc1(2)
            z_transpose(TILES - 1, 1)
            fc2(2)
            fc1(3)
            fc2(3)

        @block.vector
        def _(dve):
            def bn_stats(k, b, groups, src, stats_b, s_st):
                for n in groups:
                    nc.vector.bn_stats(stats_b[:, b, n, :], src[:, n * C:(n + 1) * C]).then_inc(s_st, 1)

            def bn_aggr(k, b, stats_b, mv_b, s_st, s_mv):
                dve.wait_ge(s_st, GRP * k + GRP)
                for n in range(GRP):
                    ins = nc.vector.bn_aggr(mv_b[:, b, n, :], stats_b[:, b, n, :])
                ins.then_inc(s_mv, 1)

            def normalise(k, b, dst, src, mv_b, rstd_b, s_done):
                for n in range(GRP):
                    ins = nc.vector.tensor_scalar(dst[:, b, n * C:(n + 1) * C], src[:, n * C:(n + 1) * C],
                                                  mv_b[:, b, n, 0:1], rstd_b[:, b, n:n + 1],
                                                  op0=ALU.subtract, op1=ALU.mult)
                ins.then_inc(s_done, 1)

            def x_of(k):
                return x_tok[:, bass.ds(k * TOK, TOK)]

            def ln1_stats(k, b):
                if isinstance(k, int):
                    dve.wait_ge(s_xtok[xtok_load(k)], 16)
                bn_stats(k, b, range(GRP), x_of(k), stats1, s_st1)

            def ln1_aggr(k, b):
                if later(k, 2):
                    dve.wait_ge(s_rstd1, k - 1)
                bn_aggr(k, b, stats1, mv1, s_st1, s_mv1)

            def ln1_apply(k, b):
                dve.wait_ge(s_rstd1, k + 1)
                if later(k, 2):
                    dve.wait_ge(s_x1, k - 1)
                normalise(k, b, xhat, x_of(k), mv1, rstd1, s_xhat)

            def ln2_stats(k, b):
                dve.wait_ge(s_yt, k + 1)
                bn_stats(k, b, range(GRP), ps_m2[:, 0:TOK], stats2, s_st2)
                bn_aggr(k, b, stats2, mv2, s_st2, s_mv2)

            def ln2_apply(k, b):
                dve.wait_ge(s_rstd2, k + 1)
                normalise(k, b, zhat, ps_m2[:, 0:TOK], mv2, rstd2, s_zhat)

            def find_max(k, b, p):
                dve.wait_ge(s_scores, k * PAIRS + p + 1)
                if later(k * PAIRS + p, 2):
                    dve.wait_ge(s_shifted, k * PAIRS + p - 1)
                nc.vector.tensor_reduce(row_max[:, p % 2, :], ps_s[p % 2][:].rearrange("q (h j) -> q h j", h=HEADS),
                                        axis=AX.X, op=ALU.max).then_inc(s_max, 1)

            def sum_rows(k, b, p):
                dve.wait_ge(s_exp, k * PAIRS + p + 1)
                nc.vector.tensor_reduce(row_sum[:, b, p, :],
                                        probs[:, p % 2, :].rearrange("q (h j) -> q h j", h=HEADS),
                                        axis=AX.X, op=ALU.add).then_inc(s_sum, 1)

            def reciprocal(k, b):
                dve.wait_ge(s_sum, PAIRS * k + PAIRS)
                if later(k, 1):
                    dve.wait_ge(s_recx, k)
                nc.vector.reciprocal(recip[:], row_sum[:, b].rearrange("q p h -> q (p h)")).then_inc(s_recip, 1)

            def normalise_attn(k, b):
                dve.wait_ge(s_pv, PAIRS * k + PAIRS)
                dve.wait_ge(s_rsb, k + 1)
                if later(k, 1):
                    dve.wait_ge(s_proj, k)
                nc.vector.tensor_tensor(attn[:].rearrange("q p w i -> q (p w i)"), ps_u[b][:], recip_t[:],
                                        op=ALU.mult).then_inc(s_attn, 1)

            def residual(k, b):
                dve.wait_ge(s_proj, k + 1)
                if not later(k, 1):
                    dve.wait_ge(s_xch, 16)
                    dve.wait_ge(s_latew, 6)
                if later(k, 2):
                    dve.wait_ge(s_yt, k - 1)
                    dve.wait_ge(s_ycopy, k - 1)
                nc.vector.scalar_tensor_tensor(y_tile[:, b, :], ps_m2[:, 0:TOK], b_out[:, 0:1],
                                               x_ch[:, bass.ds(k * TOK, TOK)],
                                               op0=ALU.add, op1=ALU.add).then_inc(s_y, 1)

            def finish(s):
                dve.wait_ge(s_fc2, s + 1)
                dve.wait_ge(s_ycopy, 2 * s + 2)
                if s >= 2:
                    dve.wait_ge(s_out[s - 2], 16)
                nc.vector.scalar_tensor_tensor(result[:, s % 2, :], ps_f[s % 2][:], vec[:, FC2B:FC2B + 1],
                                               y_all[:, s * STEP:(s + 1) * STEP],
                                               op0=ALU.add, op1=ALU.add).then_inc(s_res, 1)

            def tile(t, b):
                last = isinstance(t, int) and t == TILES - 1
                for p in range(PAIRS):
                    if p + 1 < PAIRS:
                        find_max(t, b, p + 1)
                    elif not last:
                        find_max(t + 1, 1 - b, 0)
                    if p == 2 and tile_ok(t - 1):
                        normalise_attn(t - 1, 1 - b)
                    if p == 3 and tile_ok(t - 1):
                        residual(t - 1, 1 - b)
                    sum_rows(t, b, p)
                    if p == 0 and tile_ok(t - 2):
                        ln2_stats(t - 2, b)
                    if p == 1 and tile_ok(t - 2):
                        ln2_apply(t - 2, b)
                    if p == 2 and tile_ok(t + 2):
                        ln1_apply(t + 2, b)
                    if p == 3:
                        if tile_ok(t + 3):
                            ln1_stats(t + 3, 1 - b)
                        reciprocal(t, b)
                        if tile_ok(t + 3):
                            ln1_aggr(t + 3, 1 - b)

            ln1_stats(0, 0)
            ln1_aggr(0, 0)
            dve.wait_ge(s_early, 16)
            for w in range(2):
                nc.vector.tensor_scalar(w_qkv[:, :, w * C:(w + 1) * C],
                                        w_in_t.rearrange("q (s e) -> q s e", s=3),
                                        vec[:, G1:G1 + 1], half_mask[:, w:w + 1],
                                        op0=ALU.mult, op1=ALU.mult).then_inc(s_wqkv, 1)
            ln1_apply(0, 0)
            dve.wait_ge(s_bps, 1)
            nc.vector.tensor_tensor(b_qkv[:, 0:3], ps_u[1][:, 0:3], vec[:, BQ:BQ + 3], op=ALU.add).then_inc(s_bias, 1)
            dve.wait_ge(s_bias, 1)
            nc.vector.tensor_scalar(b_qkv[:, 3:4], b_qkv[:, 0:1], float(D) ** -0.5, None,
                                    op0=ALU.mult).then_inc(s_bias, 1)
            nc.vector.tensor_scalar(minus_ident[:], ident, -1.0, None, op0=ALU.mult).then_inc(s_ident, 1)
            ln1_stats(1, 1)
            ln1_aggr(1, 1)
            dve.wait_ge(s_late, 16)
            for w in range(2):
                nc.vector.tensor_scalar(w_fc1[:, w, :], w_fc1_t, vec[:, G2:G2 + 1], half_mask[:, w:w + 1],
                                        op0=ALU.mult, op1=ALU.mult).then_inc(s_latew, 1)
            ln1_apply(1, 1)
            dve.wait_ge(s_lps, 1)
            for w in range(2):
                nc.vector.tensor_scalar(w_out[:, w, :], ps_u[1][:, 0:C], row_mask[:, w:w + 1], None,
                                        op0=ALU.mult).then_inc(s_latew, 1)
            nc.vector.tensor_tensor(b_out[:], ps_u[1][:, C:C + 1], vec[:, PROJB:PROJB + 1],
                                    op=ALU.add).then_inc(s_latew, 1)
            nc.vector.tensor_tensor(b_fc1[:], ps_u[1][:, C + 1:C + 1 + M2], vec[:, FC1B:FC1B + M2],
                                    op=ALU.add).then_inc(s_latew, 1)
            find_max(0, 0, 0)
            ln1_stats(2, 0)
            ln1_aggr(2, 0)
            all_tiles(dve, 0, tile)
            ln2_stats(TILES - 2, 0)
            normalise_attn(TILES - 1, 1)
            ln2_apply(TILES - 2, 0)
            residual(TILES - 1, 1)
            finish(0)
            ln2_stats(TILES - 1, 1)
            ln2_apply(TILES - 1, 1)
            for s in range(1, STEPS):
                finish(s)

        @block.scalar
        def _(act):
            def evacuate_xn(k, b):
                act.wait_ge(s_x1, k + 1)
                if later(k, 2):
                    act.wait_ge(s_v, k - 1)
                nc.scalar.activation(xn[:, b, :], ps_m0[:, 0:TOK], ACT.Copy).then_inc(s_xn, 1)

            def evacuate_qk(k, b):
                act.wait_ge(s_qk, k + 1)
                if later(k, 2):
                    act.wait_ge(s_scores, PAIRS * k - PAIRS)
                for w in range(2):
                    r = slice(C * w, C * w + C)
                    nc.scalar.activation(q_bd[r, b, :, w * L:(w + 1) * L],
                                         ps_m0[r, 0:TOK].rearrange("q (p i) -> q p i", p=PAIRS),
                                         ACT.Identity, bias=b_qkv[r, 3:4], scale=float(D) ** -0.5).then_inc(s_qkch, 1)
                if later(k, 2):
                    act.wait_ge(s_kmask, k - 1)
                nc.scalar.activation(k_ch[:, b, :], ps_m0[:, TOK:2 * TOK], ACT.Identity,
                                     bias=b_qkv[:, 1:2]).then_inc(s_qkch, 1)

            def evacuate_v(k, b):
                act.wait_ge(s_v, k + 1)
                nc.scalar.activation(v_ch[:], ps_m0[:, 0:TOK].rearrange("q (p i) -> q p i", p=PAIRS)
                                     .unsqueeze(2).to_broadcast([P, PAIRS, 2, L]),
                                     ACT.Identity, bias=b_qkv[:, 2:3]).then_inc(s_vch, 1)

            def evacuate_vt(k, b):
                act.wait_ge(s_vt, k + 1)
                if later(k, 2):
                    act.wait_ge(s_pv, PAIRS * k - PAIRS)
                for u in range(2):
                    r = slice(L * u, L * u + L)
                    c = slice(2 * D * u, 2 * D * u + 2 * D)
                    nc.scalar.activation(
                        v_z[r, b].rearrange("q p (a e) -> q (p a) e", e=4 * D)[:, :, c],
                        ps_m0[r, :].rearrange("q (b e) -> q b e", e=4 * D)[:, :, c],
                        ACT.Copy).then_inc(s_vz, 1)

            def exponentiate(k, b, p):
                act.wait_ge(s_shifted, k * PAIRS + p + 1)
                if later(k * PAIRS + p, 2):
                    act.wait_ge(s_pt, k * PAIRS + p - 1)
                    act.wait_ge(s_sum, k * PAIRS + p - 1)
                nc.scalar.activation(probs[:, p % 2, :], ps_s[p % 2][:], ACT.Exp).then_inc(s_exp, 1)

            def evacuate_pt(k, b, p):
                act.wait_ge(s_pt, k * PAIRS + p + 1)
                if later(k * PAIRS + p, 2):
                    act.wait_ge(s_pv, k * PAIRS + p - 1)
                nc.scalar.activation(probs_t[:, p % 2, :], ps_pt[:], ACT.Copy).then_inc(s_ptsb, 1)

            def evacuate_r(k, b):
                act.wait_ge(s_r, k + 1)
                if later(k, 1):
                    act.wait_ge(s_attn, k)
                nc.scalar.activation(recip_t[:], ps_m1[:], ACT.Copy).then_inc(s_rsb, 1)

            def evacuate_z(k, b):
                act.wait_ge(s_zt, k + 1)
                nc.scalar.activation(z_all[:, bass.ds(k * TOK, TOK)], ps_m1[:, 0:TOK], ACT.Copy).then_inc(s_z, 1)

            def gelu(s):
                for n in range(4):
                    act.wait_ge(s_fc1, 4 * s + n + 1)
                    if s >= 2:
                        act.wait_ge(s_fc2, s - 1)
                    nc.scalar.activation(hidden[:, s % 2, n, :], ps_h[n][:], ACT.Gelu,
                                         bias=b_fc1[:, n % M2:n % M2 + 1]).then_inc(s_gelu, 1)

            def tile(t, b):
                last = isinstance(t, int) and t == TILES - 1
                for p in range(PAIRS):
                    evacuate_pt(t, b, p)
                    if p + 1 < PAIRS:
                        exponentiate(t, b, p + 1)
                    elif not last:
                        exponentiate(t + 1, 1 - b, 0)
                    if p == 0:
                        if tile_ok(t + 1):
                            evacuate_qk(t + 1, 1 - b)
                        if tile_ok(t - 1):
                            evacuate_r(t - 1, 1 - b)
                    if p == 1 and tile_ok(t + 1):
                        evacuate_v(t + 1, 1 - b)
                    if p == 2 and tile_ok(t + 1):
                        evacuate_vt(t + 1, 1 - b)
                    if p == 3:
                        if tile_ok(t - 2):
                            evacuate_z(t - 2, b)
                        if tile_ok(t + 2):
                            evacuate_xn(t + 2, b)

            act.dma_start(early[:], early_d).then_inc(s_early, 16)
            evacuate_xn(0, 0)
            act.wait_ge(s_bias, 2)
            act.wait_ge(s_zero, 3)
            evacuate_qk(0, 0)
            evacuate_v(0, 0)
            evacuate_vt(0, 0)
            exponentiate(0, 0, 0)
            evacuate_xn(1, 1)
            all_tiles(act, 0, tile)
            act.wait_ge(s_latew, 6)
            evacuate_r(TILES - 1, 1)
            gelu(0)
            evacuate_z(TILES - 2, 0)
            gelu(1)
            gelu(2)
            evacuate_z(TILES - 1, 1)
            gelu(3)

        @block.gpsimd
        def _(pool):
            def rstd(k, b, mv_b, var_b, rstd_b, s_mv, s_var, s_rstd):
                pool.wait_ge(s_mv, k + 1)
                nc.gpsimd.tensor_scalar(var_b[:, b, :], mv_b[:, b, :, 1], 1.0, EPS,
                                        op0=ALU.mult, op1=ALU.add).then_inc(s_var, 1)
                pool.wait_ge(s_var, k + 1)
                nc.gpsimd.tensor_tensor(rstd_b[:, b, :], var_b[:, b, :], minus_half[:],
                                        op=ALU.pow).then_inc(s_rstd, 1)

            def rstd_1(k, b):
                rstd(k, b, mv1, var1, rstd1, s_mv1, s_var1, s_rstd1)

            def rstd_2(k, b):
                rstd(k, b, mv2, var2, rstd2, s_mv2, s_var2, s_rstd2)

            def mask_k(k, b):
                pool.wait_ge(s_qkch, 3 * k + 3)
                if not later(k, 1):
                    pool.wait_ge(s_early, 16)
                if later(k, 2):
                    pool.wait_ge(s_scores, PAIRS * k - PAIRS)
                for h in range(HEADS):
                    ins = nc.gpsimd.tensor_scalar(k_mask[:, b, :, h, :],
                                                  k_ch[:, b, :].rearrange("q (p j) -> q p j", p=PAIRS),
                                                  head_mask[:, h:h + 1], 0.0, op0=ALU.mult, op1=ALU.add)
                ins.then_inc(s_kmask, 1)

            def expand_recip(k, b):
                pool.wait_ge(s_recip, k + 1)
                if later(k, 1):
                    pool.wait_ge(s_r, k)
                nc.gpsimd.tensor_scalar(recip_x[:], recip[:].unsqueeze(2).to_broadcast([P, PAIRS * HEADS, 2 * D]),
                                        1.0, 0.0, op0=ALU.mult, op1=ALU.add).then_inc(s_recx, 1)

            def copy_y(k, b):
                pool.wait_ge(s_y, k + 1)
                nc.gpsimd.tensor_scalar(y_all[:, bass.ds(k * TOK, TOK)], y_tile[:, b, :], 1.0, 0.0,
                                        op0=ALU.mult, op1=ALU.add).then_inc(s_ycopy, 1)

            def tile(t, b):
                if tile_ok(t - 1):
                    expand_recip(t - 1, 1 - b)
                if tile_ok(t + 2):
                    rstd_1(t + 2, b)
                if tile_ok(t - 2):
                    rstd_2(t - 2, b)
                if tile_ok(t + 1):
                    mask_k(t + 1, 1 - b)
                if tile_ok(t - 1):
                    copy_y(t - 1, 1 - b)

            nc.gpsimd.memset(minus_half[:], -0.5).then_inc(s_zero, 1)
            nc.gpsimd.memset(q_bd[:], 0.0).then_inc(s_zero, 1)
            nc.gpsimd.memset(v_z[:], 0.0).then_inc(s_zero, 1)
            pool.wait_ge(s_zero, 1)
            rstd_1(0, 0)
            rstd_1(1, 1)
            mask_k(0, 0)
            all_tiles(pool, 0, tile)
            rstd_2(TILES - 2, 0)
            expand_recip(TILES - 1, 1)
            copy_y(TILES - 1, 1)
            rstd_2(TILES - 1, 1)


def kernel(**inputs):
    import concourse.bacc as bacc
    from concourse.bass_utils import run_bass_kernel_spmd

    a = {k.replace("L0_conv_", ""): np.asarray(v) for k, v in inputs.items()}
    f = a["x"].dtype
    xr = np.roll(a["x"], (-SHIFT, -SHIFT), (2, 3)).reshape(2, TILES, C, HH // WIN, WIN, WW // WIN, WIN)
    x_ch = xr.transpose(0, 2, 1, 3, 5, 4, 6).reshape(P, ALL)
    x_tok = xr.transpose(5, 4, 6, 1, 3, 0, 2).reshape(P, ALL)

    q = np.arange(P)
    ident = np.eye(P, dtype=f)
    masks = np.zeros((P, NM), f)
    masks[q, q // C] = 1
    masks[q, 2 + q % C // D] = 1
    masks[q, 10 + q // D % 2] = 1
    perm = ident.reshape(P, 2, HEADS, D).transpose(0, 2, 1, 3).reshape(P, P)

    def twice(v):
        return np.concatenate([v, v], 0)

    in_b = a["in_b"].reshape(3, C)
    vecs = np.stack([twice(a["norm1_g"]), twice(a["norm1_b"]), twice(in_b[0]), twice(in_b[1]), twice(in_b[2]),
                     twice(a["out_b"]), twice(a["proj_b"]), twice(a["norm2_g"]), twice(a["norm2_b"]),
                     twice(a["fc2_b"]), a["fc1_b"][:P], a["fc1_b"][P:]], 1)
    early = np.concatenate([ident, masks, vecs, twice(a["in_w"].T)], 1)
    out_w_x = a["out_w"].reshape(C, HEADS, 1, D).repeat(2, 2).reshape(C, P)
    proj_w_t = np.concatenate([a["proj_w"].T, a["proj_w"].T], 1)
    late = np.concatenate([perm, twice(a["fc1_w"].T),
                           a["fc2_w"].T.reshape(M2, P, C).transpose(1, 0, 2).reshape(P, M2 * C),
                           twice(out_w_x), twice(proj_w_t)], 1)

    nc = bacc.Bacc("TRN2", target_bir_lowering=False, num_devices=1)
    arrays, args = {}, []
    for name, v in (("x_tok_d", x_tok), ("x_ch_d", x_ch), ("early_d", early), ("late_d", late)):
        arrays[name] = np.ascontiguousarray(v)
        args.append(nc.dram_tensor(name, v.shape, mybir.dt.from_np(v.dtype), kind="ExternalInput").ap())
    args.append(nc.dram_tensor("out_d", (P, ALL), F32, kind="ExternalOutput").ap())
    swin_block_kernel(nc, *args)
    r = run_bass_kernel_spmd(nc, [arrays], core_ids=[0])
    out = np.asarray(r.results[0]["out_d"]).reshape(2, C, TILES, HH // WIN, WW // WIN, WIN, WIN)
    out = out.transpose(0, 2, 1, 3, 5, 4, 6).reshape(B, C, HH, WW)
    return np.roll(out, (SHIFT, SHIFT), (2, 3))
```

```python
from contextlib import ExitStack

import numpy as np

import concourse.bass as bass
from concourse import mybir

F32 = mybir.dt.float32
F32R = mybir.dt.float32r
ALU = mybir.AluOpType
ACT = mybir.ActivationFunctionType
AX = mybir.AxisListType

B, C, HH, WW = 16, 64, 16, 16
WIN, SHIFT = 8, 4
HEADS = 8
D = C // HEADS
HIDDEN = 4 * C
EPS = 1e-6
P = 128
TOK = HH * WW
TILES = B // 2
L = WIN * WIN
PAIRS = TOK // L
BLK = TOK // P
GRP = BLK * 2
M2 = HIDDEN // P
STEP = 2 * TOK
STEPS = TILES // 2
ALL = TILES * TOK
MASK_SPLIT = 5
NV = 12
G1, B1, BQ, BV, OUTB, PROJB, G2, B2, FC2B, FC1B = 0, 1, 2, 4, 5, 6, 7, 8, 9, 10
NM = 12
EARLY = P + NM + NV + 3 * C
LATE = HIDDEN + M2 * C + 3 * P


def swin_block_kernel(nc, x_tok_d, x_ch_d, early_d, late_d, out_d):
    ctx = ExitStack()
    with ctx:
        def sb(name, shape, dtype=F32):
            return ctx.enter_context(nc.sbuf_tensor(name, shape, dtype))

        def bank(name):
            return ctx.enter_context(nc.psum_tensor(name, [P, 512], F32))

        def sem(name):
            return ctx.enter_context(nc.semaphore(name))

        x_tok = sb("x_tok", [P, ALL])
        x_ch = sb("x_ch", [P, ALL])
        early = sb("early", [P, EARLY])
        late = sb("late", [P, LATE])
        ident = early[:, 0:P]
        half_mask = early[:, P:P + 2]
        head_mask = early[:, P + 2:P + 2 + HEADS]
        row_mask = early[:, P + 10:P + 12]
        vec = early[:, P + NM:P + NM + NV]
        w_in_t = early[:, P + NM + NV:EARLY]
        w_fc1_t = late[:, 0:HIDDEN]
        w_fc2_t = late[:, HIDDEN:HIDDEN + M2 * C]
        w_v_x = late[0:C, LATE - 3 * P:LATE - 2 * P]
        out_w_x = late[0:C, LATE - 2 * P:LATE - P]
        proj_w_t = late[0:C, LATE - P:LATE]

        w_qk = sb("w_qk", [P, 2, P])
        w_v = sb("w_v", [P, P])
        b_qk = sb("b_qk", [P, 3])
        b_v = sb("b_v", [P, 1])
        w_out = sb("w_out", [P, 2, C])
        b_out = sb("b_out", [P, 1])
        w_fc1 = sb("w_fc1", [P, HIDDEN])
        w_fc1_r = sb("w_fc1_r", [P, 2, HIDDEN], F32R)
        b_fc1 = sb("b_fc1", [P, M2])

        zeros = sb("zeros", [P, P])

        stats1 = sb("stats1", [P, 2, GRP, 6])
        mv1 = sb("mv1", [P, 2, GRP, 2])
        var1 = sb("var1", [P, 2, GRP])
        rstd1 = sb("rstd1", [P, 2, GRP])
        stats2 = sb("stats2", [P, 2, GRP, 6])
        mv2 = sb("mv2", [P, 2, GRP, 2])
        var2 = sb("var2", [P, 2, GRP])
        rstd2 = sb("rstd2", [P, 2, GRP])
        minus_half = sb("minus_half", [P, GRP])
        xhat = sb("xhat", [P, 2, TOK])
        zhat = sb("zhat", [P, 2, TOK])

        xn = sb("xn", [P, 2, TOK])
        q_bd = sb("q_bd", [P, 2, PAIRS, P])
        k_ch = sb("k_ch", [P, 2, TOK])
        k_mask = sb("k_mask", [P, 2, PAIRS, HEADS, L])
        v_z = sb("v_z", [P, 2, PAIRS, P])
        row_max = sb("row_max", [P, 2, HEADS], F32R)
        minus_ident = sb("minus_ident", [P, P], F32R)
        probs = sb("probs", [P, 2, 512])
        probs_t = sb("probs_t", [P, 2, 512])
        row_sum = sb("row_sum", [P, 2, PAIRS, HEADS])
        recip = sb("recip", [P, PAIRS * HEADS])
        recip_x = sb("recip_x", [P, PAIRS * HEADS, 2 * D])
        recip_t = sb("recip_t", [P, 512])
        attn = sb("attn", [P, PAIRS, 2, L])
        y_all = sb("y_all", [P, ALL])
        z_all = sb("z_all", [P, 2, ALL], F32R)

        hidden = sb("hidden", [P, 2, 4, STEP])
        result = sb("result", [P, 2, STEP])

        ps_s = [bank("ps_s0"), bank("ps_s1")]
        ps_pt = bank("ps_pt")
        ps_u = [bank("ps_u0"), bank("ps_u1")]
        ps_m0, ps_m1, ps_m2 = bank("ps_m0"), bank("ps_m1"), bank("ps_m2")
        ps_h = [ps_m0, ps_u[0], ps_s[0], ps_s[1]]
        ps_f = [ps_pt, ps_u[1]]

        early_loaded = sem("early_loaded")
        late_loaded = sem("late_loaded")
        xch_loaded = sem("xch_loaded")
        zeros_set = sem("zeros_set")
        buffers_set = sem("buffers_set")
        b_products_done = sem("b_products_done")
        b_qk_made = sem("b_qk_made")
        w_qkv_made = sem("w_qkv_made")
        minus_ident_made = sem("minus_ident_made")
        late_products_done = sem("late_products_done")
        late_weights_made = sem("late_weights_made")
        w_fc1_made = sem("w_fc1_made")
        x_stats_done = sem("x_stats_done")
        x_moments_done = sem("x_moments_done")
        x_var_done = sem("x_var_done")
        x_rstd_done = sem("x_rstd_done")
        x_centred = sem("x_centred")
        x_scaled = sem("x_scaled")
        x_transposed = sem("x_transposed")
        xn_copied = sem("xn_copied")
        qk_projected = sem("qk_projected")
        qk_copied = sem("qk_copied")
        k_masked = sem("k_masked")
        k_masked_first = sem("k_masked_first")
        v_projected = sem("v_projected")
        v_copied = sem("v_copied")
        scores_done = sem("scores_done")
        max_found = sem("max_found")
        scores_shifted = sem("scores_shifted")
        probs_done = sem("probs_done")
        rows_summed = sem("rows_summed")
        probs_transposed = sem("probs_transposed")
        probs_t_copied = sem("probs_t_copied")
        values_weighed = sem("values_weighed")
        recip_done = sem("recip_done")
        recip_expanded = sem("recip_expanded")
        recip_transposed = sem("recip_transposed")
        recip_t_copied = sem("recip_t_copied")
        attn_done = sem("attn_done")
        out_projected = sem("out_projected")
        y_done = sem("y_done")
        y_transposed = sem("y_transposed")
        y_stats_done = sem("y_stats_done")
        y_moments_done = sem("y_moments_done")
        y_var_done = sem("y_var_done")
        y_rstd_done = sem("y_rstd_done")
        y_centred = sem("y_centred")
        y_scaled = sem("y_scaled")
        z_transposed = sem("z_transposed")
        z_high_done = sem("z_high_done")
        z_low_done = sem("z_low_done")
        fc1_done = sem("fc1_done")
        gelu_done = sem("gelu_done")
        fc2_done = sem("fc2_done")
        result_done = sem("result_done")
        xtok_loaded = [sem(f"xtok_loaded{i}") for i in range(4)]
        stored = [sem(f"stored{s}") for s in range(STEPS)]

        XTOK = [(0, 1), (1, 2), (2, 4), (4, 8)]

        def xtok_load(k):
            return next(i for i, (a, b) in enumerate(XTOK) if a <= k < b)

        def columns(s):
            n = 2 if s == STEPS - 1 else 1
            return [slice(i * STEP // n, (i + 1) * STEP // n) for i in range(n)]

        def out_bank(s, i):
            return ps_m2 if i else ps_f[s % 2]

        def tile_ok(k):
            return 0 <= k < TILES

        block = ctx.enter_context(nc.Block())

        @block.sync
        def _(sp):
            for i, (a, b) in enumerate(XTOK):
                if i == 2:
                    sp.dma_start(late[:], late_d).then_inc(late_loaded, 16)
                sp.dma_start(x_tok[:, a * TOK:b * TOK], x_tok_d[:, a * TOK:b * TOK]).then_inc(xtok_loaded[i], 16)
            sp.dma_start(x_ch[:], x_ch_d).then_inc(xch_loaded, 16)
            for s in range(STEPS):
                for i, c in enumerate(columns(s)):
                    sp.wait_ge(result_done, s + 1 + i)
                    sp.dma_start(out_d[:, s * STEP + c.start:s * STEP + c.stop],
                                 result[:, s % 2, c]).then_inc(stored[s], 16)
            for s in range(STEPS):
                sp.wait_ge(stored[s], 16 * len(columns(s)))

        @block.tensor
        def _(pe):
            def scores(k, b, p):
                if k == 0 and p % 2 == 0:
                    pe.wait_ge(k_masked, p // 2 + 1)
                    pe.wait_ge(k_masked_first, p // 2 + 1)
                if k >= 1 and p == 0:
                    pe.wait_ge(k_masked, k + 2)
                if p == 0:
                    pe.wait_ge(qk_copied, 3 * k + 3)
                if k * PAIRS + p >= 2:
                    pe.wait_ge(probs_done, k * PAIRS + p - 1)
                nc.tensor.matmul(ps_s[p % 2][:], q_bd[:, b, p, :],
                                 k_mask[:, b, p].rearrange("q h j -> q (h j)"),
                                 start=True, stop=True).then_inc(scores_done, 1)

            def shift_scores(k, b, p):
                if k * PAIRS + p == 0:
                    pe.wait_ge(minus_ident_made, 1)
                pe.wait_ge(max_found, k * PAIRS + p + 1)
                nc.tensor.matmul(ps_s[p % 2][:], minus_ident[:],
                                 row_max[:, p % 2, :].unsqueeze(2).to_broadcast([P, HEADS, L]),
                                 start=False, stop=True, skip_group_check=True).then_inc(scores_shifted, 1)

            def transpose_probs(k, b, p):
                pe.wait_ge(probs_done, k * PAIRS + p + 1)
                if k * PAIRS + p >= 1:
                    pe.wait_ge(probs_t_copied, k * PAIRS + p)
                for hp in range(4):
                    ins = nc.tensor.transpose(ps_pt[:, hp * P:(hp + 1) * P],
                                              probs[:, p % 2, hp * P:(hp + 1) * P], ident)
                ins.then_inc(probs_transposed, 1)

            def weigh_values(k, b, p):
                pe.wait_ge(probs_t_copied, k * PAIRS + p + 1)
                if p == 0:
                    pe.wait_ge(v_copied, 4 * k + 4)
                    if k >= 2:
                        pe.wait_ge(attn_done, k - 1)
                for hp in range(4):
                    ins = nc.tensor.matmul(ps_u[b][32 * hp:32 * hp + 32, p * P:(p + 1) * P],
                                           v_z[:, b, p, 32 * hp:32 * hp + 32],
                                           probs_t[:, p % 2, hp * P:(hp + 1) * P],
                                           start=True, stop=True, tile_position=(0, 32 * hp))
                ins.then_inc(values_weighed, 1)

            def x_transpose(k, b):
                pe.wait_ge(x_scaled, k + 1)
                if k >= 1:
                    pe.wait_ge(v_copied, 4 * k)
                for n in range(BLK):
                    ins = nc.tensor.transpose(ps_m0[:, n * P:(n + 1) * P],
                                              xhat[:, b, n * P:(n + 1) * P], ident)
                ins.then_inc(x_transposed, 1)

            def project_qk(k, b):
                pe.wait_ge(xn_copied, k + 1)
                for i in range(2):
                    ins = nc.tensor.matmul(ps_m0[:, i * TOK:(i + 1) * TOK], w_qk[:, i, :], xn[:, b, :],
                                           start=True, stop=True)
                ins.then_inc(qk_projected, 1)

            def project_v(k, b):
                pe.wait_ge(qk_copied, 3 * k + 3)
                for n in range(BLK):
                    ins = nc.tensor.matmul(ps_m0[:, n * P:(n + 1) * P], xn[:, b, n * P:(n + 1) * P], w_v[:],
                                           start=True, stop=True)
                ins.then_inc(v_projected, 1)

            def recip_transpose(k, b):
                pe.wait_ge(recip_expanded, k + 1)
                if k >= 2:
                    pe.wait_ge(z_low_done, 2 * k - 2)
                for p in range(PAIRS):
                    ins = nc.tensor.transpose(
                        ps_m1[:, p * P:(p + 1) * P],
                        recip_x[:, p * HEADS:(p + 1) * HEADS, :].rearrange("q h e -> q (h e)"), ident)
                ins.then_inc(recip_transposed, 1)

            def project_out(k, b):
                pe.wait_ge(attn_done, k + 1)
                if k == 0:
                    pe.wait_ge(late_weights_made, 2)
                if k >= 1:
                    pe.wait_ge(y_centred, k)
                for w in range(2):
                    ins = nc.tensor.matmul(ps_m2[C * w:C * w + C, 0:TOK], w_out[:, w, :], attn[:, :, w, :],
                                           start=True, stop=True)
                ins.then_inc(out_projected, 1)

            def y_transpose(k, b):
                pe.wait_ge(y_done, k + 1)
                for n in range(BLK):
                    ins = nc.tensor.transpose(ps_m2[:, n * P:(n + 1) * P],
                                              y_all[:, k * TOK + n * P:k * TOK + (n + 1) * P], ident)
                ins.then_inc(y_transposed, 1)

            def z_transpose(k, b):
                pe.wait_ge(y_scaled, k + 1)
                pe.wait_ge(recip_t_copied, k + 1 + tile_ok(k + 1))
                for n in range(BLK):
                    ins = nc.tensor.transpose(ps_m1[:, n * P:(n + 1) * P],
                                              zhat[:, b, n * P:(n + 1) * P], ident)
                ins.then_inc(z_transposed, 1)

            def fc1(s, ns=range(4)):
                pe.wait_ge(z_low_done, 4 * s + 4)
                if s == 0:
                    pe.wait_ge(w_fc1_made, 3)
                for n in ns:
                    w, m = n // M2, n % M2
                    if s >= 1:
                        pe.wait_ge(gelu_done, 4 * (s - 1) + n + 1)
                    for part in range(2):
                        ins = nc.tensor.matmul(ps_h[n][:], w_fc1_r[:, part, m * P:(m + 1) * P],
                                               z_all[:, w, s * STEP:(s + 1) * STEP],
                                               start=(part == 0), stop=(part == 1))
                    ins.then_inc(fc1_done, 1)

            def fc2(s):
                if s >= 2:
                    pe.wait_ge(result_done, s - 1)
                pe.wait_ge(gelu_done, 4 * s + 4)
                for i, c in enumerate(columns(s)):
                    for m in range(M2):
                        for w in range(2):
                            ins = nc.tensor.matmul(out_bank(s, i)[C * w:C * w + C, c], w_fc2_t[:, m * C:(m + 1) * C],
                                                   hidden[:, s % 2, w * M2 + m, c],
                                                   start=(m == 0), stop=(m == M2 - 1))
                    ins.then_inc(fc2_done, 1)

            def bias_of_v():
                pe.wait_ge(late_weights_made, 5)
                for w in range(2):
                    ins = nc.tensor.matmul(ps_m2[C * w:C * w + C, C + 4:C + 5], w_out[:, w, :], b_v[:],
                                           start=True, stop=True)
                ins.then_inc(late_products_done, 1)

            def tile(t, b):
                last = t == TILES - 1
                for p in range(PAIRS):
                    nk, nb, np_ = (t, b, p + 1) if p + 1 < PAIRS else (t + 1, 1 - b, 0)
                    more = not (last and p == PAIRS - 1)
                    if more and (t, p) != (0, 0):
                        scores(nk, nb, np_)
                    if last and p == PAIRS - 1:
                        fc1(0, range(1))
                        project_out(t - 1, 1 - b)
                    transpose_probs(t, b, p)
                    if p >= 1:
                        weigh_values(t, b, p - 1)
                    elif tile_ok(t - 1):
                        weigh_values(t - 1, 1 - b, PAIRS - 1)
                    if p == 0:
                        if tile_ok(t + 1):
                            project_qk(t + 1, 1 - b)
                    if p == 1:
                        if tile_ok(t - 2):
                            y_transpose(t - 2, b)
                        if tile_ok(t - 1):
                            recip_transpose(t - 1, 1 - b)
                    if p == 2 and tile_ok(t + 1):
                        project_v(t + 1, 1 - b)
                    if p == 2 and t == 0:
                        bias_of_v()
                    if p == 3:
                        if tile_ok(t - 1) and not last:
                            project_out(t - 1, 1 - b)
                        if tile_ok(t + 2):
                            x_transpose(t + 2, b)
                        if tile_ok(t - 2):
                            z_transpose(t - 2, b)
                    if more:
                        shift_scores(nk, nb, np_)

            def warm_up(products):
                for _ in range(products):
                    nc.tensor.matmul(ps_pt[:, 0:P], zeros[:], zeros[:], start=True, stop=True)

            pe.wait_ge(zeros_set, 1)
            warm_up(6)
            pe.wait_ge(early_loaded, 16)
            for i in range(2):
                for w in range(2):
                    ins = nc.tensor.matmul(ps_u[1][C * w:C * w + C, i:i + 1], w_in_t[0:C, i * C:(i + 1) * C],
                                           vec[0:C, B1:B1 + 1], start=True, stop=True)
            ins.then_inc(b_products_done, 1)
            warm_up(4)
            x_transpose(0, 0)
            warm_up(2)
            pe.wait_ge(w_qkv_made, 4)
            project_qk(0, 0)
            pe.wait_ge(late_loaded, 16)
            nc.tensor.matmul(ps_m2[:, 0:C], out_w_x, proj_w_t[:, 0:C], start=True, stop=True)
            nc.tensor.matmul(ps_m2[:, C:C + 1], proj_w_t, vec[0:C, OUTB:OUTB + 1],
                             start=True, stop=True)
            for m in range(M2):
                nc.tensor.matmul(ps_m2[:, C + 1 + m:C + 2 + m], w_fc1_t[0:C, m * P:(m + 1) * P],
                                 vec[0:C, B2:B2 + 1], start=True, stop=True)
            nc.tensor.matmul(ps_m2[:, C + 3:C + 4], w_v_x, vec[0:C, B1:B1 + 1],
                             start=True, stop=True).then_inc(late_products_done, 1)
            warm_up(4)
            scores(0, 0, 0)
            project_v(0, 0)
            scores(0, 0, 1)
            shift_scores(0, 0, 0)
            x_transpose(1, 1)
            for t in range(TILES):
                tile(t, t % 2)
            weigh_values(TILES - 1, 1, PAIRS - 1)
            y_transpose(TILES - 2, 0)
            fc1(0, range(1, 2))
            recip_transpose(TILES - 1, 1)
            fc1(0, range(2, 4))
            fc1(1, range(1))
            project_out(TILES - 1, 1)
            z_transpose(TILES - 2, 0)
            fc1(1, range(1, 3))
            y_transpose(TILES - 1, 1)
            fc1(1, range(3, 4))
            fc2(0)
            fc1(2, range(2))
            z_transpose(TILES - 1, 1)
            fc1(2, range(2, 4))
            fc2(1)
            fc1(3)
            fc2(2)
            fc2(3)

        @block.vector
        def _(dve):
            def bn_stats(k, b, groups, src, stats_b, stats_done):
                for n in groups:
                    nc.vector.bn_stats(stats_b[:, b, n, :], src[:, n * C:(n + 1) * C]).then_inc(stats_done, 1)

            def bn_aggr(k, b, stats_b, mv_b, stats_done, moments_done):
                dve.wait_ge(stats_done, GRP * k + GRP)
                for n in range(GRP):
                    ins = nc.vector.bn_aggr(mv_b[:, b, n, :], stats_b[:, b, n, :])
                ins.then_inc(moments_done, 1)

            def groups(ap):
                return ap.rearrange("q (n c) -> q n c", n=GRP)

            def centre(k, b, dst, src, mv_b, moments_done, centred):
                dve.wait_ge(moments_done, k + 1)
                nc.vector.tensor_tensor(groups(dst[:, b, :]), groups(src),
                                        mv_b[:, b, :, 0:1].to_broadcast([P, GRP, C]),
                                        op=ALU.subtract).then_inc(centred, 1)

            def scale(k, b, dst, rstd_b, centred, rstd_done, scaled):
                dve.wait_ge(centred, k + 1)
                dve.wait_ge(rstd_done, k + 1)
                nc.vector.tensor_tensor(groups(dst[:, b, :]), groups(dst[:, b, :]),
                                        rstd_b[:, b, :].unsqueeze(2).to_broadcast([P, GRP, C]),
                                        op=ALU.mult).then_inc(scaled, 1)

            def x_of(k):
                return x_tok[:, k * TOK:(k + 1) * TOK]

            def ln1_stats(k, b):
                dve.wait_ge(xtok_loaded[xtok_load(k)], 16)
                bn_stats(k, b, range(GRP), x_of(k), stats1, x_stats_done)

            def ln1_aggr(k, b):
                if k >= 2:
                    dve.wait_ge(x_rstd_done, k - 1)
                bn_aggr(k, b, stats1, mv1, x_stats_done, x_moments_done)

            def ln1_centre(k, b):
                if k >= 2:
                    dve.wait_ge(x_transposed, k - 1)
                centre(k, b, xhat, x_of(k), mv1, x_moments_done, x_centred)

            def ln1_scale(k, b):
                scale(k, b, xhat, rstd1, x_centred, x_rstd_done, x_scaled)

            def ln2_stats(k, b):
                dve.wait_ge(y_transposed, k + 1)
                bn_stats(k, b, range(GRP), ps_m2[:, 0:TOK], stats2, y_stats_done)
                bn_aggr(k, b, stats2, mv2, y_stats_done, y_moments_done)

            def ln2_centre(k, b):
                if k >= 2:
                    dve.wait_ge(z_transposed, k - 1)
                centre(k, b, zhat, ps_m2[:, 0:TOK], mv2, y_moments_done, y_centred)

            def ln2_scale(k, b):
                scale(k, b, zhat, rstd2, y_centred, y_rstd_done, y_scaled)

            def z_low(k, b):
                for w in range(2):
                    dve.wait_ge(z_high_done, 2 * k + w + 1)
                    nc.vector.tensor_tensor(z_all[C:P, w, k * TOK:(k + 1) * TOK], ps_m1[w * C:(w + 1) * C, 0:TOK],
                                            z_all[0:C, w, k * TOK:(k + 1) * TOK],
                                            op=ALU.subtract).then_inc(z_low_done, 1)

            def find_max(k, b, p):
                dve.wait_ge(scores_done, k * PAIRS + p + 1)
                if k * PAIRS + p >= 2:
                    dve.wait_ge(scores_shifted, k * PAIRS + p - 1)
                nc.vector.tensor_reduce(row_max[:, p % 2, :], ps_s[p % 2][:].rearrange("q (h j) -> q h j", h=HEADS),
                                        axis=AX.X, op=ALU.max).then_inc(max_found, 1)

            def sum_rows(k, b, p):
                dve.wait_ge(probs_done, k * PAIRS + p + 1)
                nc.vector.tensor_reduce(row_sum[:, b, p, :],
                                        probs[:, p % 2, :].rearrange("q (h j) -> q h j", h=HEADS),
                                        axis=AX.X, op=ALU.add).then_inc(rows_summed, 1)

            def reciprocal(k, b):
                dve.wait_ge(rows_summed, PAIRS * k + PAIRS)
                if k >= 1:
                    dve.wait_ge(recip_expanded, k)
                nc.vector.reciprocal(recip[:], row_sum[:, b].rearrange("q p h -> q (p h)")).then_inc(recip_done, 1)

            def normalise_attn(k, b):
                dve.wait_ge(values_weighed, PAIRS * k + PAIRS)
                dve.wait_ge(recip_t_copied, k + 1)
                if k >= 1:
                    dve.wait_ge(out_projected, k)
                nc.vector.tensor_tensor(attn[:].rearrange("q p w i -> q (p w i)"), ps_u[b][:], recip_t[:],
                                        op=ALU.mult).then_inc(attn_done, 1)

            def residual(k, b):
                dve.wait_ge(out_projected, k + 1)
                if k == 0:
                    dve.wait_ge(xch_loaded, 16)
                    dve.wait_ge(late_weights_made, 6)
                nc.vector.scalar_tensor_tensor(y_all[:, k * TOK:(k + 1) * TOK], ps_m2[:, 0:TOK], b_out[:, 0:1],
                                               x_ch[:, k * TOK:(k + 1) * TOK],
                                               op0=ALU.add, op1=ALU.add).then_inc(y_done, 1)

            def finish(s):
                dve.wait_ge(y_done, 2 * s + 2)
                if s >= 2:
                    dve.wait_ge(stored[s - 2], 16)
                for i, c in enumerate(columns(s)):
                    dve.wait_ge(fc2_done, s + 1 + i)
                    nc.vector.scalar_tensor_tensor(result[:, s % 2, c], out_bank(s, i)[:, c], vec[:, FC2B:FC2B + 1],
                                                   y_all[:, s * STEP + c.start:s * STEP + c.stop],
                                                   op0=ALU.add, op1=ALU.add).then_inc(result_done, 1)

            def tile(t, b):
                last = t == TILES - 1
                for p in range(PAIRS):
                    if p + 1 < PAIRS:
                        find_max(t, b, p + 1)
                    elif not last:
                        find_max(t + 1, 1 - b, 0)
                    if p == 0:
                        if tile_ok(t - 2):
                            residual(t - 2, b)
                        if tile_ok(t - 3):
                            z_low(t - 3, 1 - b)
                    if p == 2:
                        if tile_ok(t - 1):
                            normalise_attn(t - 1, 1 - b)
                        if tile_ok(t - 2):
                            ln2_centre(t - 2, b)
                    if p == 3 and tile_ok(t - 2):
                        ln2_scale(t - 2, b)
                    sum_rows(t, b, p)
                    if t == 0 and p == 1:
                        late_weights()
                    if t == 0 and p == 3:
                        late_bias()
                    if t == 1 and p == 1:
                        dve.wait_ge(late_loaded, 16)
                        split_fc1()
                    if p == 1:
                        if tile_ok(t - 2):
                            ln2_stats(t - 2, b)
                        if tile_ok(t + 2):
                            ln1_centre(t + 2, b)
                    if p == 2 and tile_ok(t + 2):
                        ln1_scale(t + 2, b)
                    if p == 3:
                        reciprocal(t, b)
                        if tile_ok(t + 3):
                            ln1_stats(t + 3, 1 - b)
                            ln1_aggr(t + 3, 1 - b)

            def late_weights():
                dve.wait_ge(late_products_done, 1)
                for w in range(2):
                    nc.vector.tensor_scalar(w_out[:, w, :], ps_m2[:, 0:C], row_mask[:, w:w + 1], None,
                                            op0=ALU.mult).then_inc(late_weights_made, 1)
                nc.vector.tensor_tensor(b_fc1[:], ps_m2[:, C + 1:C + 1 + M2], vec[:, FC1B:FC1B + M2],
                                        op=ALU.add).then_inc(late_weights_made, 1)
                nc.vector.tensor_tensor(b_out[:], ps_m2[:, C:C + 1], vec[:, PROJB:PROJB + 1],
                                        op=ALU.add).then_inc(late_weights_made, 1)
                nc.vector.tensor_tensor(b_v[:], ps_m2[:, C + 3:C + 4], vec[:, BV:BV + 1],
                                        op=ALU.add).then_inc(late_weights_made, 1)

            def late_bias():
                dve.wait_ge(late_weights_made, 4)
                dve.wait_ge(late_products_done, 2)
                nc.vector.tensor_tensor(b_out[:], b_out[:], ps_m2[:, C + 4:C + 5], op=ALU.add).then_inc(late_weights_made, 1)

            def split_fc1():
                nc.vector.tensor_scalar(w_fc1[:], w_fc1_t, vec[:, G2:G2 + 1], None, op0=ALU.mult).then_inc(w_fc1_made, 1)
                dve.wait_ge(w_fc1_made, 1)
                nc.vector.tensor_copy(w_fc1_r[:, 0, :], w_fc1[:]).then_inc(w_fc1_made, 1)
                dve.wait_ge(w_fc1_made, 2)
                nc.vector.tensor_tensor(w_fc1_r[:, 1, :], w_fc1[:], w_fc1_r[:, 0, :], op=ALU.subtract).then_inc(w_fc1_made, 1)

            def mask_k_first(half):
                dve.wait_ge(qk_copied, 1)
                for h in range(MASK_SPLIT):
                    ins = nc.vector.tensor_scalar(k_mask[:, 0, 2 * half:2 * half + 2, h, :],
                                                  k_ch[:, 0, half * P:(half + 1) * P].rearrange("q (p j) -> q p j", p=2),
                                                  head_mask[:, h:h + 1], None, op0=ALU.mult)
                ins.then_inc(k_masked_first, 1)

            nc.vector.memset(zeros[:], 0.0).then_inc(zeros_set, 1)
            ln1_stats(0, 0)
            ln1_aggr(0, 0)
            ln1_centre(0, 0)
            dve.wait_ge(early_loaded, 16)
            for w in range(2):
                nc.vector.tensor_scalar(w_qk[:, :, w * C:(w + 1) * C],
                                        w_in_t[:, 0:2 * C].rearrange("q (s e) -> q s e", s=2),
                                        vec[:, G1:G1 + 1], half_mask[:, w:w + 1],
                                        op0=ALU.mult, op1=ALU.mult).then_inc(w_qkv_made, 1)
            ln1_scale(0, 0)
            for w in range(2):
                nc.vector.tensor_scalar(w_v[:].rearrange("q (h w d) -> q h w d", w=2, d=D)[:, :, w, :],
                                        w_in_t[:, 2 * C:3 * C].rearrange("q (h d) -> q h d", d=D),
                                        vec[:, G1:G1 + 1], half_mask[:, w:w + 1],
                                        op0=ALU.mult, op1=ALU.mult).then_inc(w_qkv_made, 1)
            dve.wait_ge(b_products_done, 1)
            nc.vector.tensor_tensor(b_qk[:, 0:2], ps_u[1][:, 0:2], vec[:, BQ:BQ + 2], op=ALU.add).then_inc(b_qk_made, 1)
            dve.wait_ge(b_qk_made, 1)
            nc.vector.tensor_scalar(b_qk[:, 2:3], b_qk[:, 0:1], float(D) ** -0.5, None,
                                    op0=ALU.mult).then_inc(b_qk_made, 1)
            nc.vector.tensor_scalar(minus_ident[:], ident, -1.0, None, op0=ALU.mult).then_inc(minus_ident_made, 1)
            ln1_stats(1, 1)
            ln1_aggr(1, 1)
            ln1_centre(1, 1)
            mask_k_first(0)
            ln1_scale(1, 1)
            mask_k_first(1)
            find_max(0, 0, 0)
            ln1_stats(2, 0)
            ln1_aggr(2, 0)
            for t in range(TILES):
                tile(t, t % 2)
            residual(TILES - 2, 0)
            z_low(TILES - 3, 1)
            ln2_stats(TILES - 2, 0)
            ln2_centre(TILES - 2, 0)
            normalise_attn(TILES - 1, 1)
            ln2_scale(TILES - 2, 0)
            residual(TILES - 1, 1)
            z_low(TILES - 2, 0)
            ln2_stats(TILES - 1, 1)
            ln2_centre(TILES - 1, 1)
            ln2_scale(TILES - 1, 1)
            finish(0)
            z_low(TILES - 1, 1)
            finish(1)
            finish(2)
            finish(3)

        @block.scalar
        def _(act):
            def evacuate_xn(k, b):
                act.wait_ge(x_transposed, k + 1)
                if k >= 2:
                    act.wait_ge(v_projected, k - 1)
                nc.scalar.activation(xn[:, b, :], ps_m0[:, 0:TOK], ACT.Copy).then_inc(xn_copied, 1)

            def evacuate_k(k, b):
                act.wait_ge(qk_projected, k + 1)
                if k >= 2:
                    act.wait_ge(k_masked, k)
                nc.scalar.activation(k_ch[:, b, :], ps_m0[:, TOK:2 * TOK], ACT.Identity,
                                     bias=b_qk[:, 1:2]).then_inc(qk_copied, 1)

            def evacuate_q(k, b):
                if k >= 2:
                    act.wait_ge(scores_done, PAIRS * k - PAIRS)
                for w in range(2):
                    r = slice(C * w, C * w + C)
                    nc.scalar.activation(q_bd[r, b, :, w * L:(w + 1) * L],
                                         ps_m0[r, 0:TOK].rearrange("q (p i) -> q p i", p=PAIRS),
                                         ACT.Identity, bias=b_qk[r, 2:3], scale=float(D) ** -0.5).then_inc(qk_copied, 1)

            def evacuate_v(k, b):
                act.wait_ge(v_projected, k + 1)
                if k >= 2:
                    act.wait_ge(values_weighed, PAIRS * k - PAIRS)
                for r in range(2):
                    for u in range(2):
                        c = slice(2 * D * u, 2 * D * u + 2 * D)
                        nc.scalar.activation(
                            v_z[L * u:L * u + L, b].rearrange("q (n r) (a e) -> q r n a e", r=2, e=4 * D)[:, r, :, :, c],
                            ps_m0[L * r:L * r + L, 0:TOK].rearrange("q (n a e) -> q n a e", n=BLK, e=4 * D)[:, :, :, c],
                            ACT.Copy).then_inc(v_copied, 1)

            def exponentiate(k, b, p):
                act.wait_ge(scores_shifted, k * PAIRS + p + 1)
                if k * PAIRS + p >= 2:
                    act.wait_ge(probs_transposed, k * PAIRS + p - 1)
                    act.wait_ge(rows_summed, k * PAIRS + p - 1)
                nc.scalar.activation(probs[:, p % 2, :], ps_s[p % 2][:], ACT.Exp).then_inc(probs_done, 1)

            def evacuate_pt(k, b, p):
                act.wait_ge(probs_transposed, k * PAIRS + p + 1)
                if k * PAIRS + p >= 2:
                    act.wait_ge(values_weighed, k * PAIRS + p - 1)
                nc.scalar.activation(probs_t[:, p % 2, :], ps_pt[:], ACT.Copy).then_inc(probs_t_copied, 1)

            def evacuate_r(k, b):
                act.wait_ge(recip_transposed, k + 1)
                if k >= 1:
                    act.wait_ge(attn_done, k)
                nc.scalar.activation(recip_t[:], ps_m1[:], ACT.Copy).then_inc(recip_t_copied, 1)

            def evacuate_z(k, b):
                act.wait_ge(z_transposed, k + 1)
                for w in range(2):
                    nc.scalar.activation(z_all[0:C, w, k * TOK:(k + 1) * TOK], ps_m1[w * C:(w + 1) * C, 0:TOK],
                                         ACT.Copy).then_inc(z_high_done, 1)

            def gelu(s, ns=range(4)):
                for n in ns:
                    act.wait_ge(fc1_done, 4 * s + n + 1)
                    if s >= 2:
                        act.wait_ge(fc2_done, s - 1)
                    nc.scalar.activation(hidden[:, s % 2, n, :], ps_h[n][:], ACT.Gelu,
                                         bias=b_fc1[:, n % M2:n % M2 + 1]).then_inc(gelu_done, 1)

            def tile(t, b):
                last = t == TILES - 1
                for p in range(PAIRS):
                    evacuate_pt(t, b, p)
                    if p == 0 and tile_ok(t + 1):
                        evacuate_k(t + 1, 1 - b)
                    if p + 1 < PAIRS:
                        exponentiate(t, b, p + 1)
                    elif not last:
                        exponentiate(t + 1, 1 - b, 0)
                    if p == 1 and tile_ok(t - 1):
                        evacuate_r(t - 1, 1 - b)
                    if p == 0 and tile_ok(t + 1):
                        evacuate_q(t + 1, 1 - b)
                    if p == 2 and tile_ok(t + 1):
                        evacuate_v(t + 1, 1 - b)
                    if p == 3:
                        if tile_ok(t + 2):
                            evacuate_xn(t + 2, b)
                        if tile_ok(t - 2):
                            evacuate_z(t - 2, b)

            act.dma_start(early[:], early_d).then_inc(early_loaded, 16)
            evacuate_xn(0, 0)
            act.wait_ge(b_qk_made, 2)
            act.wait_ge(buffers_set, 3)
            evacuate_k(0, 0)
            evacuate_q(0, 0)
            evacuate_v(0, 0)
            exponentiate(0, 0, 0)
            evacuate_xn(1, 1)
            for t in range(TILES):
                tile(t, t % 2)
            act.wait_ge(late_weights_made, 3)
            gelu(0, range(1))
            evacuate_r(TILES - 1, 1)
            gelu(0, range(1, 4))
            evacuate_z(TILES - 2, 0)
            gelu(1)
            gelu(2, range(2))
            evacuate_z(TILES - 1, 1)
            gelu(2, range(2, 4))
            gelu(3)

        @block.gpsimd
        def _(pool):
            def rstd(k, b, mv_b, var_b, rstd_b, moments_done, var_done, rstd_done):
                pool.wait_ge(moments_done, k + 1)
                nc.gpsimd.tensor_scalar(var_b[:, b, :], mv_b[:, b, :, 1], 1.0, EPS,
                                        op0=ALU.mult, op1=ALU.add).then_inc(var_done, 1)
                pool.wait_ge(var_done, k + 1)
                nc.gpsimd.tensor_tensor(rstd_b[:, b, :], var_b[:, b, :], minus_half[:],
                                        op=ALU.pow).then_inc(rstd_done, 1)

            def rstd_1(k, b):
                rstd(k, b, mv1, var1, rstd1, x_moments_done, x_var_done, x_rstd_done)

            def rstd_2(k, b):
                rstd(k, b, mv2, var2, rstd2, y_moments_done, y_var_done, y_rstd_done)

            def mask_k(k, b, pairs, heads):
                pool.wait_ge(qk_copied, 3 * k + 1)
                if k >= 2:
                    pool.wait_ge(scores_done, PAIRS * k - PAIRS)
                n = len(pairs)
                for h in heads:
                    ins = nc.gpsimd.tensor_scalar(
                        k_mask[:, b, pairs[0]:pairs[0] + n, h, :],
                        k_ch[:, b, pairs[0] * L:(pairs[0] + n) * L].rearrange("q (p j) -> q p j", p=n),
                        head_mask[:, h:h + 1], 0.0, op0=ALU.mult, op1=ALU.add)
                ins.then_inc(k_masked, 1)

            def expand_recip(k, b):
                pool.wait_ge(recip_done, k + 1)
                if k >= 1:
                    pool.wait_ge(recip_transposed, k)
                nc.gpsimd.tensor_scalar(recip_x[:], recip[:].unsqueeze(2).to_broadcast([P, PAIRS * HEADS, 2 * D]),
                                        1.0, 0.0, op0=ALU.mult, op1=ALU.add).then_inc(recip_expanded, 1)

            def tile(t, b):
                if tile_ok(t - 1):
                    expand_recip(t - 1, 1 - b)
                if tile_ok(t + 2):
                    rstd_1(t + 2, b)
                if tile_ok(t + 1):
                    mask_k(t + 1, 1 - b, range(PAIRS), range(HEADS))
                if tile_ok(t - 2):
                    rstd_2(t - 2, b)

            nc.gpsimd.memset(minus_half[:], -0.5).then_inc(buffers_set, 1)
            nc.gpsimd.memset(q_bd[:], 0.0).then_inc(buffers_set, 1)
            nc.gpsimd.memset(v_z[:], 0.0).then_inc(buffers_set, 1)
            pool.wait_ge(buffers_set, 1)
            rstd_1(0, 0)
            rstd_1(1, 1)
            pool.wait_ge(early_loaded, 16)
            mask_k(0, 0, range(0, 2), range(MASK_SPLIT, HEADS))
            mask_k(0, 0, range(2, 4), range(MASK_SPLIT, HEADS))
            for t in range(TILES):
                tile(t, t % 2)
            expand_recip(TILES - 1, 1)
            rstd_2(TILES - 2, 0)
            rstd_2(TILES - 1, 1)


def kernel(**inputs):
    import concourse.bacc as bacc
    from concourse.bass_utils import run_bass_kernel_spmd

    a = {k.replace("L0_conv_", ""): np.asarray(v) for k, v in inputs.items()}
    f = a["x"].dtype
    xr = np.roll(a["x"], (-SHIFT, -SHIFT), (2, 3)).reshape(2, TILES, C, HH // WIN, WIN, WW // WIN, WIN)
    x_ch = xr.transpose(0, 2, 1, 3, 5, 4, 6).reshape(P, ALL)
    x_tok = xr.transpose(5, 4, 6, 1, 3, 0, 2).reshape(P, ALL)

    q = np.arange(P)
    ident = np.eye(P, dtype=f)
    masks = np.zeros((P, NM), f)
    masks[q, q // C] = 1
    masks[q, 2 + q % C // D] = 1
    masks[q, 10 + q // D % 2] = 1

    def heads_twice(v):
        return v.reshape(-1, HEADS, 1, D).repeat(2, 2).reshape(-1, P)

    def twice(v):
        return np.concatenate([v, v], 0)

    in_b = a["in_b"].reshape(3, C)
    vecs = np.stack([twice(a["norm1_g"]), twice(a["norm1_b"]), twice(in_b[0]), twice(in_b[1]), heads_twice(in_b[2])[0],
                     twice(a["out_b"]), twice(a["proj_b"]), twice(a["norm2_g"]), twice(a["norm2_b"]),
                     twice(a["fc2_b"]), a["fc1_b"][:P], a["fc1_b"][P:]], 1)
    early = np.concatenate([ident, masks, vecs, twice(a["in_w"].T)], 1)
    proj_w_t = np.concatenate([a["proj_w"].T, a["proj_w"].T], 1)
    late = np.concatenate([twice(a["fc1_w"].T),
                           a["fc2_w"].T.reshape(M2, P, C).transpose(1, 0, 2).reshape(P, M2 * C),
                           twice(heads_twice(a["in_w"][2 * C:].T)), twice(heads_twice(a["out_w"])),
                           twice(proj_w_t)], 1)

    nc = bacc.Bacc("TRN2", target_bir_lowering=False, num_devices=1)
    arrays, args = {}, []
    for name, v in (("x_tok_d", x_tok), ("x_ch_d", x_ch), ("early_d", early), ("late_d", late)):
        arrays[name] = np.ascontiguousarray(v)
        args.append(nc.dram_tensor(name, v.shape, mybir.dt.from_np(v.dtype), kind="ExternalInput").ap())
    args.append(nc.dram_tensor("out_d", (P, ALL), F32, kind="ExternalOutput").ap())
    swin_block_kernel(nc, *args)
    r = run_bass_kernel_spmd(nc, [arrays], core_ids=[0])
    out = np.asarray(r.results[0]["out_d"]).reshape(2, C, TILES, HH // WIN, WW // WIN, WIN, WIN)
    out = out.transpose(0, 2, 1, 3, 5, 4, 6).reshape(B, C, HH, WW)
    return np.roll(out, (SHIFT, SHIFT), (2, 3))
```
